# Optimizing a Trainium2 kernel written in Bass

```python
import numpy as np
import jax
import jax.numpy as jnp

def _softmax(x, axis=-1):
    return jax.nn.softmax(x, axis=axis)

def _gelu(x):
    return jax.nn.gelu(x, approximate=True)

def _silu(x):
    return jax.nn.silu(x)

def _sigmoid(x):
    return jax.nn.sigmoid(x)

def _layernorm(x, axis=-1, eps=1e-05):
    m = jnp.mean(x, axis=axis, keepdims=True)
    v = jnp.var(x, axis=axis, keepdims=True)
    return (x - m) / jnp.sqrt(v + eps)

def _scatter_add(tgt, idx, src, axis=0):
    return tgt.at[idx].add(src)

def _segment_sum(src, seg, n):
    return jax.ops.segment_sum(src, seg, n)
kernel_name = 'mk_macaron_d1_jaxref_r8_9ff5e4'

def setup_inputs(seed: int=0):
    np.random.seed(seed)
    _w = jnp.asarray

    def _L0_attn_setup():
        import jax, jax.numpy as jnp
        import numpy as np
        import math
        D_MODEL = 128
        N_HEADS = 16
        HEAD_DIM = D_MODEL // N_HEADS
        LAMBDA_INIT = 0.8 - 0.6 * math.exp(-0.3 * 0)
        EPS = 1e-06

        def _rope_cache(seq_len, head_dim, dtype):
            half = head_dim // 2
            inv_freq = 1.0 / 10000.0 ** (jnp.arange(half, dtype=jnp.float32) / max(half, 1))
            ang = jnp.arange(seq_len, dtype=jnp.float32)[:, None] * inv_freq[None, :]
            return (jnp.cos(ang).astype(dtype)[None, None], jnp.sin(ang).astype(dtype)[None, None])

        def _apply_rope(x, cos, sin):
            half = x.shape[-1] // 2
            x1, x2 = (x[..., :half], x[..., half:])
            return jnp.concatenate([x1 * cos - x2 * sin, x1 * sin + x2 * cos], axis=-1)
        key = jax.random.key(seed)
        ks = jax.random.split(key, 16)
        B, S, D = (2, 256, D_MODEL)
        s = 0.02
        return {'x': jax.random.normal(ks[0], (B, S, D), jnp.float32), 'Wq': jax.random.normal(ks[1], (2 * D, D), jnp.float32) * s, 'bq': jnp.zeros((2 * D,), jnp.float32), 'Wk': jax.random.normal(ks[2], (2 * D, D), jnp.float32) * s, 'bk': jnp.zeros((2 * D,), jnp.float32), 'Wv': jax.random.normal(ks[3], (D, D), jnp.float32) * s, 'bv': jnp.zeros((D,), jnp.float32), 'Wo': jax.random.normal(ks[4], (D, D), jnp.float32) * s, 'bo': jnp.zeros((D,), jnp.float32), 'head_norm_w': jnp.ones((N_HEADS, HEAD_DIM), jnp.float32), 'lq1': jax.random.normal(ks[5], (N_HEADS, HEAD_DIM), jnp.float32) * 0.1, 'lk1': jax.random.normal(ks[6], (N_HEADS, HEAD_DIM), jnp.float32) * 0.1, 'lq2': jax.random.normal(ks[7], (N_HEADS, HEAD_DIM), jnp.float32) * 0.1, 'lk2': jax.random.normal(ks[8], (N_HEADS, HEAD_DIM), jnp.float32) * 0.1}
    _L0_attn_in = _L0_attn_setup()

    def _L0_ffn_setup():
        import jax, jax.numpy as jnp
        import numpy as np
        DIM = 128
        NUM_EXPERTS = 8
        ACTIVE_EXPERTS = 2
        EXPERT_DIM = 256
        key = jax.random.key(seed)
        k1, k2, k3, k4 = jax.random.split(key, 4)
        x = jax.random.normal(k1, (1, 256, DIM), dtype=jnp.float32)
        gate_w = jax.random.normal(k2, (NUM_EXPERTS, DIM), dtype=jnp.float32) * 0.02
        balance_bias = jnp.zeros((NUM_EXPERTS,), dtype=jnp.float32)
        w1 = jax.random.normal(k3, (NUM_EXPERTS, EXPERT_DIM, DIM), dtype=jnp.float32) * 0.02
        w2 = jax.random.normal(k4, (NUM_EXPERTS, DIM, EXPERT_DIM), dtype=jnp.float32) * 0.02
        return {'x': x, 'gate_w': gate_w, 'balance_bias': balance_bias, 'w1': w1, 'w2': w2}
    _L0_ffn_in = _L0_ffn_setup()
    _d = {'L0_attn_x': _L0_attn_in['x'], 'L0_attn_Wq': _L0_attn_in['Wq'], 'L0_attn_bq': _L0_attn_in['bq'], 'L0_attn_Wk': _L0_attn_in['Wk'], 'L0_attn_bk': _L0_attn_in['bk'], 'L0_attn_Wv': _L0_attn_in['Wv'], 'L0_attn_bv': _L0_attn_in['bv'], 'L0_attn_Wo': _L0_attn_in['Wo'], 'L0_attn_bo': _L0_attn_in['bo'], 'L0_attn_head_norm_w': _L0_attn_in['head_norm_w'], 'L0_attn_lq1': _L0_attn_in['lq1'], 'L0_attn_lk1': _L0_attn_in['lk1'], 'L0_attn_lq2': _L0_attn_in['lq2'], 'L0_attn_lk2': _L0_attn_in['lk2'], 'L0_ffn_gate_w': _L0_ffn_in['gate_w'], 'L0_ffn_balance_bias': _L0_ffn_in['balance_bias'], 'L0_ffn_w1': _L0_ffn_in['w1'], 'L0_ffn_w2': _L0_ffn_in['w2']}
    _x0 = _d['L0_attn_x']
    _d['L0_attn_x'] = jax.random.normal(jax.random.fold_in(jax.random.key(seed), 1), (32, 256, 128), dtype=_x0.dtype)
    del _x0
    return _d

def reference(L0_attn_x, L0_attn_Wq, L0_attn_bq, L0_attn_Wk, L0_attn_bk, L0_attn_Wv, L0_attn_bv, L0_attn_Wo, L0_attn_bo, L0_attn_head_norm_w, L0_attn_lq1, L0_attn_lk1, L0_attn_lq2, L0_attn_lk2, L0_ffn_gate_w, L0_ffn_balance_bias, L0_ffn_w1, L0_ffn_w2):

    def _L0_attn_ref(x, Wq, bq, Wk, bk, Wv, bv, Wo, bo, head_norm_w, lq1, lk1, lq2, lk2):
        import jax, jax.numpy as jnp
        import numpy as np
        import math
        D_MODEL = 128
        N_HEADS = 16
        HEAD_DIM = D_MODEL // N_HEADS
        LAMBDA_INIT = 0.8 - 0.6 * math.exp(-0.3 * 0)
        EPS = 1e-06

        def _rope_cache(seq_len, head_dim, dtype):
            half = head_dim // 2
            inv_freq = 1.0 / 10000.0 ** (jnp.arange(half, dtype=jnp.float32) / max(half, 1))
            ang = jnp.arange(seq_len, dtype=jnp.float32)[:, None] * inv_freq[None, :]
            return (jnp.cos(ang).astype(dtype)[None, None], jnp.sin(ang).astype(dtype)[None, None])

        def _apply_rope(x, cos, sin):
            half = x.shape[-1] // 2
            x1, x2 = (x[..., :half], x[..., half:])
            return jnp.concatenate([x1 * cos - x2 * sin, x1 * sin + x2 * cos], axis=-1)
        B, S, D = x.shape
        H, hd = (N_HEADS, HEAD_DIM)
        dtype = x.dtype
        q = (x @ Wq.T + bq).reshape(B, S, H, 2 * hd).transpose(0, 2, 1, 3)
        k = (x @ Wk.T + bk).reshape(B, S, H, 2 * hd).transpose(0, 2, 1, 3)
        v = (x @ Wv.T + bv).reshape(B, S, H, hd).transpose(0, 2, 1, 3)
        q1, q2 = (q[..., :hd], q[..., hd:])
        k1, k2 = (k[..., :hd], k[..., hd:])
        cos, sin = _rope_cache(S, hd, dtype)
        q1, q2 = (_apply_rope(q1, cos, sin), _apply_rope(q2, cos, sin))
        k1, k2 = (_apply_rope(k1, cos, sin), _apply_rope(k2, cos, sin))
        scale = 1.0 / math.sqrt(hd)
        s1 = jnp.einsum('bhqd,bhkd->bhqk', q1, k1) * scale
        s2 = jnp.einsum('bhqd,bhkd->bhqk', q2, k2) * scale
        causal = jnp.triu(jnp.ones((S, S), bool), k=1)
        neg = jnp.finfo(dtype).min
        s1 = jnp.where(causal, neg, s1)
        s2 = jnp.where(causal, neg, s2)
        a1 = jax.nn.softmax(s1, axis=-1)
        a2 = jax.nn.softmax(s2, axis=-1)
        lam = LAMBDA_INIT + jnp.exp(jnp.sum(lq1 * lk1, -1)) - jnp.exp(jnp.sum(lq2 * lk2, -1))
        attn = a1 - lam.astype(dtype)[None, :, None, None] * a2
        out = jnp.einsum('bhqk,bhkd->bhqd', attn, v)
        rms = jnp.mean(out * out, axis=-1, keepdims=True)
        out = out * jax.lax.rsqrt(rms + EPS)
        out = out * head_norm_w[None, :, None, :]
        out = out * (1.0 - LAMBDA_INIT)
        out = out.transpose(0, 2, 1, 3).reshape(B, S, D)
        return out @ Wo.T + bo

    def _L0_ffn_ref(x, gate_w, balance_bias, w1, w2):
        import jax, jax.numpy as jnp
        import numpy as np
        DIM = 128
        NUM_EXPERTS = 8
        ACTIVE_EXPERTS = 2
        EXPERT_DIM = 256
        B, S, D = x.shape
        T = B * S
        xf = x.reshape(T, D)
        gate_logits = jnp.einsum('td,ed->te', xf, gate_w)
        gate_scores = jax.nn.sigmoid(gate_logits + balance_bias)
        topk_scores, topk_idx = jax.lax.top_k(gate_scores, ACTIVE_EXPERTS)
        topk_scores = topk_scores / (topk_scores.sum(axis=-1, keepdims=True) + 1e-06)
        comb = jnp.zeros((T, NUM_EXPERTS), dtype=x.dtype)
        comb = comb.at[jnp.arange(T)[:, None], topk_idx].add(topk_scores)
        h = jax.nn.silu(jnp.einsum('td,ehd->teh', xf, w1))
        expert_out = jnp.einsum('teh,edh->ted', h, w2)
        out = jnp.einsum('te,ted->td', comb, expert_out)
        return out.reshape(B, S, D)
    x = L0_attn_x
    x = x + 0.5 * _L0_ffn_ref(_layernorm(x, axis=-1), L0_ffn_gate_w, L0_ffn_balance_bias, L0_ffn_w1, L0_ffn_w2)
    x = x + _L0_attn_ref(_layernorm(x, axis=-1), L0_attn_Wq, L0_attn_bq, L0_attn_Wk, L0_attn_bk, L0_attn_Wv, L0_attn_bv, L0_attn_Wo, L0_attn_bo, L0_attn_head_norm_w, L0_attn_lq1, L0_attn_lk1, L0_attn_lq2, L0_attn_lk2)
    x = x + 0.5 * _L0_ffn_ref(_layernorm(x, axis=-1), L0_ffn_gate_w, L0_ffn_balance_bias, L0_ffn_w1, L0_ffn_w2)
    return x

_drawn_inputs = setup_inputs


def setup_inputs(seed=0):
    import zlib

    import numpy as np

    out = dict(_drawn_inputs(seed))
    spreads = {'L0_attn_bq': (0.0, 0.8),
     'L0_attn_bk': (0.0, 0.8),
     'L0_attn_bv': (0.0, 0.1),
     'L0_attn_bo': (0.0, 0.1),
     'L0_attn_head_norm_w': (1.0, 0.2),
     'L0_ffn_balance_bias': (0.0, 2.0)}
    factors = {'L0_attn_Wq': 8.0,
     'L0_attn_Wk': 8.0,
     'L0_attn_lq1': 8.0,
     'L0_attn_lk1': 8.0,
     'L0_attn_lq2': 8.0,
     'L0_attn_lk2': 8.0,
     'L0_ffn_gate_w': 25.721}
    for name, (base, spread) in spreads.items():
        noise = np.random.default_rng([zlib.crc32(name.encode()), seed]).standard_normal(out[name].shape)
        drawn = base * np.exp(spread * noise) if base else spread * noise
        out[name] = jnp.asarray(drawn.astype(out[name].dtype))
    for name, factor in factors.items():
        out[name] = (out[name] * factor).astype(out[name].dtype)
    return out
```

```python
import math
from contextlib import ExitStack

import numpy as np

import concourse.bass as bass
from concourse import mybir

F32 = mybir.dt.float32
BF16 = mybir.dt.bfloat16
U32 = mybir.dt.uint32
ALU = mybir.AluOpType
ACT = mybir.ActivationFunctionType
AX = mybir.AxisListType

P = 128
D = 128
B, S = 32, 256
T = B * S
H, HD = 16, 8
HS = 2 * H
LAMBDA_INIT = 0.8 - 0.6 * math.exp(-0.3 * 0)
RMS_EPS = 1e-6
LN_EPS = 1e-5
SCALE = 1.0 / math.sqrt(HD)
E, EH = 8, 256
MASKED = -1e30


def wait(engine, semaphore, count):
    if isinstance(count, int) and count <= 0:
        return
    engine.wait_ge(semaphore, count)


def wait_apart(engine, semaphore, count):
    wait(engine, semaphore, count)
    engine.nop(nofuse=True)



FT = 512
FB = T // FT
FTT = FT // P
HC = E * EH // P
NHT = 8
NUP = 4
NYW = 4


def ffn(nc, tag, x_in, x_out, w):
    with ExitStack() as ctx:
        def sb(name, shape, dt=F32):
            return ctx.enter_context(nc.sbuf_tensor(f"{tag}_{name}", shape, dt))

        def ps(name, shape, dt=F32):
            return ctx.enter_context(nc.psum_tensor(f"{tag}_{name}", shape, dt))

        def sem(name):
            return ctx.enter_context(nc.semaphore(f"{tag}_{name}"))

        w1 = sb("w1", [P, E * EH])
        w2 = sb("w2", [P, HC, D])
        gate_w = sb("gate_w", [P, E])
        gate_b = sb("gate_b", [P, E])
        ident = sb("ident", [P, P])
        iota = sb("iota", [P, E])
        e_const = sb("e_const", [P, FTT * E])
        minus_half = sb("minus_half", [P, FTT])
        x = sb("x", [P, 2, FTT, D])
        stats = sb("stats", [P, FTT, 6])
        mean_var = sb("mean_var", [P, FTT, 2])
        var_eps = sb("var_eps", [P, FTT])
        rstd = sb("rstd", [P, FTT])
        xn = sb("xn", [P, FTT, D])
        xt = sb("xt", [P, 2, FT])
        nz = sb("nz", [P, FTT, E])
        ez = sb("ez", [P, FTT, E])
        score = sb("score", [P, FTT, E])
        rest = sb("rest", [P, FTT, E])
        pick1 = sb("pick1", [P, FTT, E])
        pick2 = sb("pick2", [P, FTT, E])
        picked = sb("picked", [P, FTT, E])
        top = sb("top", [P, 2, FTT, 8])
        top_at = sb("top_at", [P, 2, FTT, 8], U32)
        top_atf = sb("top_atf", [P, 2, FTT])
        denom = sb("denom", [P, FTT])
        rdenom = sb("rdenom", [P, FTT])
        comb = sb("comb", [P, 2, FTT, E])
        ht = sb("ht", [P, NHT, FT])
        yw = sb("yw", [P, NYW, FTT, D])
        acc = sb("acc", [P, 2, FTT, D])

        up = ps("up", [P, NUP, FT])
        y = ps("y", [P, 2, FTT, D])
        xt_ps = ps("xt_ps", [P, FT])
        gate_ps = ps("gate_ps", [P, FTT, E])

        weights_in = sem("weights_in")
        const_step = sem("const_step")
        x_in_s = [sem(f"x_in{k}") for k in range(2)]
        stored = sem("stored")
        ln_step = sem("ln_step")
        rstd_ready = sem("rstd_ready")
        xn_ready = sem("xn_ready")
        transposed = sem("transposed")
        xt_ready = sem("xt_ready")
        logits_done = sem("logits_done")
        z_ready = sem("z_ready")
        ez_ready = sem("ez_ready")
        gate_step = sem("gate_step")
        comb_ready = sem("comb_ready")
        up_done = sem("up_done")
        hidden_ready = sem("hidden_ready")
        expert_done = sem("expert_done")
        weighted = sem("weighted")
        added = sem("added")

        LN, GATE = 3, 16

        def at(r, c, per=1, add=0):
            return r * (2 * per) + (c * per + add)

        def blocks(engine, body):
            body(0, 0, True)
            body(0, 1, True)
            with engine.Fori(0, FB // 2 - 2) as r:
                body(r, 2, True)
                body(r, 3, True)
            body(FB // 2 - 2, 2, True)
            body(FB // 2 - 2, 3, False)

        with nc.Block() as block:

            @block.sync
            def _(sp):
                sp.dma_start(x[:, 0], x_in[0:FT, :].rearrange("(t p) d -> p t d", p=P)).then_inc(x_in_s[0], 16)
                for dst, src in ((gate_w[:], w["gate_w"]), (gate_b[:], w["gate_b"].partition_broadcast(P)), (w1[:], w["w1"]), (w2[:], w["w2"])):
                    sp.dma_start(dst, src).then_inc(weights_in, 16)

                def body(r, c, more):
                    if more:
                        wait_apart(sp, added, at(r, c, E))
                        sp.dma_start(x[:, (c + 1) % 2], x_in[bass.ds(at(r, c + 1, FT), FT), :]
                                     .rearrange("(t p) d -> p t d", p=P)).then_inc(x_in_s[(c + 1) % 2], 16)
                    wait_apart(sp, stored, at(r, c, 16))
                    wait_apart(sp, added, at(r, c, E, E))
                    sp.dma_start(x_out[bass.ds(at(r, c, FT), FT), :].rearrange("(t p) d -> p t d", p=P),
                                 acc[:, c % 2]).then_inc(stored, 16)

                blocks(sp, body)
                sp.wait_ge(stored, 16 * FB)

            @block.gpsimd
            def _(pool):
                nc.gpsimd.memset(ident[:], 0.0).then_inc(const_step, 1)
                nc.gpsimd.memset(e_const[:], math.e)
                nc.gpsimd.memset(minus_half[:], -0.5)
                nc.gpsimd.iota(iota[:], pattern=[[1, E]], base=0, channel_multiplier=0,
                               allow_small_or_imprecise_dtypes=True).then_inc(const_step, 1)
                pool.wait_ge(const_step, 2)
                nc.gpsimd.affine_select(out=ident[:], in_=ident[:], compare_op=ALU.not_equal, fill=1.0,
                                        base=0, pattern=[[-1, P]], channel_multiplier=1).then_inc(const_step, 1)

                def ln_rstd(r, c):
                    wait(pool, ln_step, at(r, c, LN, 3))
                    nc.gpsimd.tensor_tensor(rstd[:], var_eps[:], minus_half[:], ALU.pow).then_inc(rstd_ready, 1)

                def gate_exp(r, c, part):
                    wait(pool, z_ready, at(r, c, 1, 1))
                    k = slice(part * FTT // 2, (part + 1) * FTT // 2)
                    n = FTT * E // 2
                    nc.gpsimd.tensor_tensor(ez[:, k].rearrange("p t e -> p (t e)"), e_const[:, 0:n],
                                            nz[:, k].rearrange("p t e -> p (t e)"), ALU.pow).then_inc(ez_ready, 1)

                ln_rstd(0, 0)
                gate_exp(0, 0, 0)
                gate_exp(0, 0, 1)

                def body(r, c, more):
                    total = acc[:, c % 2]
                    for e in range(E):
                        wait(pool, weighted, at(r, c, E, e + 1))
                        wait(pool, added, at(r, c, E, e))
                        if e == 0:
                            wait(pool, x_in_s[c % 2], (r + c // 2 + 1) * 16)
                            wait(pool, stored, at(r, c, 16, -16))
                        nc.gpsimd.tensor_tensor(total, yw[:, e % NYW], x[:, c % 2] if e == 0 else total,
                                                ALU.add).then_inc(added, 1)
                        if more and e == 0:
                            ln_rstd(r, c + 1)
                        if more and e in (4, 5):
                            gate_exp(r, c + 1, e - 4)

                blocks(pool, body)

            @block.scalar
            def _(act):
                def xt_copy(r, c):
                    wait(act, transposed, at(r, c, 1, 1))
                    nc.scalar.activation(xt[:, c % 2], xt_ps[:], ACT.Copy).then_inc(xt_ready, 1)

                xt_copy(0, 0)

                def body(r, c, more):
                    for k in range(HC):
                        wait(act, up_done, at(r, c, HC, k + 1))
                        wait(act, expert_done, at(r, c, E, (k - NHT) // 2 + 1))
                        nc.scalar.activation(ht[:, k % NHT], up[:, k % NUP],
                                             ACT.Silu).then_inc(hidden_ready, 1)
                        if more and k == 9:
                            xt_copy(r, c + 1)

                blocks(act, body)

            @block.vector
            def _(dve):
                def ln_stats(r, c):
                    wait(dve, x_in_s[c % 2], (r + c // 2 + 1) * 16)
                    for t in range(FTT):
                        last = nc.vector.bn_stats(stats[:, t], x[:, c % 2, t])
                    last.then_inc(ln_step, 1)
                    wait_apart(dve, ln_step, at(r, c, LN, 1))
                    for t in range(FTT):
                        last = nc.vector.bn_aggr(mean_var[:, t], stats[:, t])
                    last.then_inc(ln_step, 1)
                    wait(dve, ln_step, at(r, c, LN, 2))
                    nc.vector.tensor_scalar(var_eps[:], mean_var[:, :, 1], LN_EPS, None, ALU.add).then_inc(ln_step, 1)

                def normalise(r, c):
                    wait(dve, rstd_ready, at(r, c, 1, 1))
                    wait(dve, transposed, at(r, c))
                    for t in range(FTT):
                        last = nc.vector.tensor_scalar(xn[:, t], x[:, c % 2, t], mean_var[:, t, 0:1],
                                                       rstd[:, t:t + 1], ALU.subtract, ALU.mult)
                    last.then_inc(xn_ready, 1)

                def logits(r, c):
                    wait(dve, logits_done, at(r, c, 1, 1))
                    nc.vector.scalar_tensor_tensor(out=nz[:], in0=gate_ps[:], scalar=-1.0,
                                                   in1=gate_b[:].unsqueeze(1).to_broadcast([P, FTT, E]),
                                                   op0=ALU.mult, op1=ALU.subtract).then_inc(z_ready, 1)

                def gate(r, c):
                    done = [0]

                    def step(instruction):
                        done[0] += 1
                        instruction.then_inc(gate_step, 1)
                        wait_apart(dve, gate_step, at(r, c, GATE, done[0]))

                    wait(dve, ez_ready, at(r, c, 2, 2))
                    step(nc.vector.tensor_scalar(rest[:], ez[:], 1.0, None, ALU.add))
                    step(nc.vector.reciprocal(score[:], rest[:]))
                    for n, (scores, pick) in enumerate(((score, pick1), (rest, pick2))):
                        for t in range(FTT):
                            last = nc.vector.max(top[:, n, t], scores[:, t])
                        step(last)
                        for t in range(FTT):
                            last = nc.vector.max_index(top_at[:, n, t], top[:, n, t], scores[:, t])
                        step(last)
                        step(nc.vector.tensor_copy(top_atf[:, n], top_at[:, n, :, 0]))
                        step(nc.vector.tensor_tensor(pick[:], iota[:].unsqueeze(1).to_broadcast([P, FTT, E]),
                                                     top_atf[:, n].unsqueeze(2).to_broadcast([P, FTT, E]),
                                                     ALU.is_equal))
                        if n == 0:
                            step(nc.vector.scalar_tensor_tensor(out=rest[:], in0=pick1[:], scalar=-2.0, in1=score[:],
                                                                op0=ALU.mult, op1=ALU.add))
                    step(nc.vector.tensor_tensor(picked[:], pick1[:], pick2[:], ALU.add))
                    step(nc.vector.tensor_tensor(denom[:], top[:, 0, :, 0], top[:, 1, :, 0], ALU.add))
                    step(nc.vector.tensor_scalar(denom[:], denom[:], 1e-6, 2.0, ALU.add, ALU.mult))
                    step(nc.vector.reciprocal(rdenom[:], denom[:]))
                    nc.vector.tensor_tensor(picked[:], picked[:], score[:], ALU.mult).then_inc(gate_step, 1)
                    wait(dve, gate_step, at(r, c, GATE, done[0] + 1))
                    nc.vector.tensor_tensor(comb[:, c % 2], picked[:],
                                            rdenom[:].unsqueeze(2).to_broadcast([P, FTT, E]),
                                            ALU.mult).then_inc(comb_ready, 1)

                dve.wait_ge(weights_in, 64)
                dve.wait_ge(const_step, 2)
                ln_stats(0, 0)
                normalise(0, 0)
                logits(0, 0)
                gate(0, 0)

                def body(r, c, more):
                    for e in range(E):
                        wait(dve, expert_done, at(r, c, E, e + 1))
                        wait(dve, added, at(r, c, E, e - NYW + 1))
                        if e == 0:
                            wait(dve, comb_ready, at(r, c, 1, 1))
                        nc.vector.tensor_tensor(yw[:, e % NYW], y[:, e % 2],
                                                comb[:, c % 2, :, e:e + 1].to_broadcast([P, FTT, D]),
                                                ALU.mult).then_inc(weighted, 1)
                        if more and e == 0:
                            ln_stats(r, c + 1)
                        if more and e == 1:
                            normalise(r, c + 1)
                        if more and e == 4:
                            logits(r, c + 1)
                        if more and e == 7:
                            gate(r, c + 1)

                blocks(dve, body)

            @block.tensor
            def _(pe):
                def transpose_x(r, c):
                    wait(pe, xn_ready, at(r, c, 1, 1))
                    wait(pe, xt_ready, at(r, c))
                    for t in range(FTT):
                        last = nc.tensor.transpose(xt_ps[:, t * P:(t + 1) * P], xn[:, t], ident[:])
                    last.then_inc(transposed, 1)

                def gate_logits(r, c):
                    wait(pe, xt_ready, at(r, c, 1, 1))
                    wait(pe, z_ready, at(r, c))
                    for t in range(FTT):
                        last = nc.tensor.matmul(gate_ps[:, t], xt[:, c % 2, t * P:(t + 1) * P], gate_w[:],
                                                start=True, stop=True)
                    last.then_inc(logits_done, 1)

                pe.wait_ge(const_step, 3)
                pe.wait_ge(weights_in, 64)
                transpose_x(0, 0)
                gate_logits(0, 0)

                def down(r, c, e):
                    wait(pe, hidden_ready, at(r, c, HC, 2 * e + 2))
                    wait(pe, weighted, at(r, c, E, e - 1))
                    for t in range(FTT):
                        for k in (2 * e, 2 * e + 1):
                            last = nc.tensor.matmul(y[:, e % 2, t], ht[:, k % NHT, t * P:(t + 1) * P], w2[:, k],
                                                    start=(k % 2 == 0), stop=(k % 2 == 1))
                    last.then_inc(expert_done, 1)

                def body(r, c, more):
                    for e in range(E):
                        for k in (2 * e, 2 * e + 1):
                            wait(pe, hidden_ready, at(r, c, HC, k - NUP + 1))
                            nc.tensor.matmul(up[:, k % NUP], w1[:, k * P:(k + 1) * P], xt[:, c % 2],
                                             start=True, stop=True).then_inc(up_done, 1)
                        if e:
                            down(r, c, e - 1)
                        if more and e == 3:
                            transpose_x(r, c + 1)
                        if more and e == 5:
                            gate_logits(r, c + 1)
                    down(r, c, E - 1)

                blocks(pe, body)



NSLOT = 3
NP = 6
TERMS = ((0, 0), (0, 1), (0, 2), (1, 0), (1, 1), (2, 0))
ROWS = len(TERMS) * HD
AUG = 52
QB = S // P
NC4 = 4
VW = 32

ORDER = [("XT", 0), ("S", 0), ("QK", 0), ("S", 1), ("QK", 1), ("S", 2), ("V", 0), ("NT", 0), ("S", 3), ("T", 0),
         ("NT", 1), ("T", 1), ("S", 4), ("T", 2), ("S", 5), ("T", 3), ("S", 6), ("T", 4), ("S", 7), ("T", 5),
         ("S", 8), ("T", 6), ("S", 9), ("T", 7), ("OT", 0), ("S", 10), ("T", 8), ("S", 11), ("T", 9), ("OP", 0),
         ("NM", 0), ("T", 10), ("T", 11)]
UNITS = {"XT": 1, "QK": 2, "V": 1, "S": 12, "T": 12, "NT": 2, "OT": 1, "OP": 1, "NM": 1}
OFFSET = {"XT": 1, "QK": 1, "V": 1, "S": 0, "NM": 0, "T": -1, "NT": -2, "OT": -2, "OP": -2}


class Turn:

    def __init__(self, r, c, looped):
        self.r, self.c, self.looped = r, c, looped

    def runs(self, off):
        return self.looped or 0 <= self.c + off < B

    def at(self, off, per=1, add=0):
        return self.r * (3 * per) + ((self.c + off) * per + add)

    def slot(self, off):
        return (self.c + off) % NSLOT

    def uses(self, off, per=1):
        return self.r * per + ((self.c + off) // NSLOT + 1) * per


def turns(engine, body, first):
    start = 3
    for i in range(first, start):
        body(Turn(0, i, False))
    n = (B - 2 - start) // NSLOT
    with engine.Fori(0, n) as r:
        for k in range(NSLOT):
            body(Turn(r, start + k, True))
    for i in range(start + NSLOT * n, B + 2):
        body(Turn(0, i, False))


def attention(nc, tag, x_in, x_out, w):
    stack_q = nc.dram_tensor(f"{tag}_stack_q", (NSLOT, 2, AUG, H, S), BF16).ap()
    stack_k = nc.dram_tensor(f"{tag}_stack_k", (NSLOT, 2, AUG, H, S), BF16).ap()
    max_rows = nc.dram_tensor(f"{tag}_max_rows", (NSLOT, 2 * 3 * H, S), BF16).ap()
    with ExitStack() as ctx:
        def sb(name, shape, dt=F32):
            return ctx.enter_context(nc.sbuf_tensor(f"{tag}_{name}", shape, dt))

        def ps(name, shape, dt=F32):
            return ctx.enter_context(nc.psum_tensor(f"{tag}_{name}", shape, dt))

        def sem(name):
            return ctx.enter_context(nc.semaphore(f"{tag}_{name}"))

        wqk = sb("wqk", [P, 2 * NC4, P])
        bqk = sb("bqk", [P, 2 * NC4])
        wv = sb("wv", [P, D])
        bv = sb("bv", [P, D])
        wo = sb("wo", [P, D])
        bo = sb("bo", [P, D])
        rope = sb("rope", [P, 2, S])
        norm_w = sb("norm_w", [P, D])
        lam_in = sb("lam_in", [P, 4, D])
        lam_prod = sb("lam_prod", [P, 2, D])
        lam_sum = sb("lam_sum", [P, 2, H])
        lam_exp = sb("lam_exp", [P, 2, H])
        stream_w = sb("stream_w", [P, H, 2])
        ident = sb("ident", [P, P])
        ident16 = sb("ident16", [P, P], BF16)
        mask = sb("mask", [P, 2, P], BF16)
        one_rows = sb("one_rows", [16, 3, H * S // 16], BF16)
        zero_rows = sb("zero_rows", [16, 4, H * S // 16], BF16)
        minus_half = sb("minus_half", [P, QB])

        x = sb("x", [P, NSLOT, QB, D])
        xr = sb("xr", [P, NSLOT, QB, D])
        xrb = sb("xrb", [P, QB, D])
        xo = sb("xo", [P, NSLOT, QB, D])
        stats = sb("stats", [P, QB, 6])
        mean_var = sb("mean_var", [P, QB, 2])
        var_eps = sb("var_eps", [P, QB])
        rstd = sb("rstd", [P, QB])
        xn = sb("xn", [P, QB, D])
        xt = sb("xt", [P, S])
        turned = sb("turned", [P, 2, 2, 2 * S])
        qk = sb("qk", [P, 2, 2 * S])
        left = sb("left", [P, 2, 2 * S])
        parts = sb("parts", [P, 2, 3, 2 * S], BF16)
        qs = sb("qs", [2 * AUG, NSLOT, H, S], BF16)
        kd = sb("kd", [2 * AUG, NSLOT, H, 2, S], BF16)
        v = sb("v", [P, NSLOT, QB, H, VW])
        nmax = sb("nmax", [P, QB, HS])
        nmax_left = sb("nmax_left", [P, QB, HS])
        nmax_parts = sb("nmax_parts", [P, QB, 2, 3, H], BF16)
        nmax_t = sb("nmax_t", [2 * 3 * H, S], BF16)
        prob = sb("prob", [P, NP, 1024])
        o_t = sb("o_t", [P, 4, 2, S])
        rsum = sb("rsum", [P, QB, HS])
        rsum_w = sb("rsum_w", [P, QB, HS])
        o_w = sb("o_w", [P, QB, HS, HD])
        o = sb("o", [P, QB, H, HD])
        o_sq = sb("o_sq", [P, QB, H, HD])
        ms = sb("ms", [P, QB * H])
        ms_eps = sb("ms_eps", [P, QB * H])
        ln_ms = sb("ln_ms", [P, QB * H])
        y0 = sb("y0", [P, QB * H])
        newton = sb("newton", [P, QB * H])
        newton2 = sb("newton2", [P, QB * H])
        rrms = sb("rrms", [P, QB * H])
        o_n = sb("o_n", [P, QB, H, HD])
        o_f = sb("o_f", [P, QB, D])
        of_t = sb("of_t", [P, S])

        ring = ps("ring", [P, 3, 1024])
        o_ps = ps("o_ps", [P, 2, 2, S])

        weights_in = sem("weights_in")
        rows_in = sem("rows_in")
        setup = sem("setup")
        dve_setup = sem("dve_setup")
        lam_ready = sem("lam_ready")
        lam_sums = sem("lam_sums")
        lam_step = sem("lam_step")
        ms_ready = sem("ms_ready")
        x_in_s = [sem(f"x_in{k}") for k in range(NSLOT)]
        xr_in = [sem(f"xr_in{k}") for k in range(NSLOT)]
        stored = sem("stored")
        stack_out = sem("stack_out")
        stack_in = [sem(f"stack_in{k}") for k in range(NSLOT)]
        max_out = sem("max_out")
        max_in = sem("max_in")
        ln_step = sem("ln_step")
        rstd_ready = sem("rstd_ready")
        xn_ready = sem("xn_ready")
        pe = {kind: sem(f"{kind}_computed") for kind in UNITS}
        read = {kind: sem(f"{kind}_read") for kind in UNITS}
        qk_ready = sem("qk_ready")
        hi_ready = sem("hi_ready")
        left_step = sem("left_step")
        mid_ready = sem("mid_ready")
        max_step = sem("max_step")
        masked = sem("masked")
        prob_ready = sem("prob_ready")
        pv_done = sem("pv_done")
        o_copied = sem("o_copied")
        norm_step = sem("norm_step")
        rms_step = sem("rms_step")
        pool_norm = sem("pool_norm")
        NORM = 11

        def wait_unit(engine, turn, kind, n):
            wait(engine, pe[kind], turn.at(OFFSET[kind], UNITS[kind], n + 1))

        with nc.Block() as block:

            @block.sync
            def _(sp):
                def load_x(turn):
                    wait_apart(sp, xn_ready, turn.at(2 - NSLOT, 1, 1))
                    sp.dma_start(x[:, turn.slot(2)], x_in[bass.ds(turn.at(2, S), S), :]
                                 .rearrange("(t p) d -> p t d", p=P)).then_inc(x_in_s[turn.slot(2)], 16)

                load_x(Turn(0, -2, False))
                for name, dst in (("wqk", wqk), ("bqk", bqk), ("wv", wv), ("wo", wo), ("rope", rope)):
                    sp.dma_start(dst[:], w[name]).then_inc(weights_in, 16)
                for name, dst in (("bv", bv), ("bo", bo), ("norm_w", norm_w)):
                    sp.dma_start(dst[:], w[name].partition_broadcast(P)).then_inc(weights_in, 16)
                for n, name in enumerate(("lq1", "lk1", "lq2", "lk2")):
                    sp.dma_start(lam_in[:, n], w[name].partition_broadcast(P)).then_inc(weights_in, 16)
                sp.wait_ge(dve_setup, 2)
                for k in range(NSLOT):
                    for s in range(2):
                        sp.dma_start(stack_k[k, s, ROWS:ROWS + 3].rearrange("r h q -> r (h q)")
                                     .rearrange("r (p n) -> p r n", p=16), one_rows[:]).then_inc(rows_in, 16)
                        sp.dma_start(stack_k[k, s, ROWS + 3:AUG].rearrange("r h q -> r (h q)")
                                     .rearrange("r (p n) -> p r n", p=16), zero_rows[:, 0:1]).then_inc(rows_in, 16)
                        sp.dma_start(stack_q[k, s, ROWS:AUG].rearrange("r h q -> r (h q)")
                                     .rearrange("r (p n) -> p r n", p=16), zero_rows[:]).then_inc(rows_in, 16)

                def body(turn):
                    if turn.runs(2) and not (turn.c == -2 and not turn.looped):
                        load_x(turn)
                    if turn.runs(-2):
                        wait_apart(sp, read["OP"], turn.at(-3, 1, 1))
                        sp.dma_start(xr[:, turn.slot(-2)], x_in[bass.ds(turn.at(-2, S), S), :]
                                     .rearrange("(t p) d -> p t d", p=P)).then_inc(xr_in[turn.slot(-2)], 16)
                    if turn.runs(1):
                        k = turn.slot(1)
                        for n, dst in ((0, stack_q), (1, stack_k)):
                            wait_apart(sp, left_step, turn.at(1, 4, 3 + n))
                            for term, part in enumerate(t[n] for t in TERMS):
                                rows = dst[k, :, term * HD:(term + 1) * HD].rearrange("s d (pp c) q -> s (d pp) (c q)", c=2)
                                sp.dma_start(rows, parts[:, n, part]).then_inc(stack_out, 16)
                        wait_apart(sp, stack_out, turn.at(1, 16 * 2 * len(TERMS), 16 * 2 * len(TERMS)))
                        sp.wait_ge(rows_in, 16 * 6 * NSLOT)
                        wait_apart(sp, pe["T"], turn.at(1 - NSLOT, 12, 12))
                        sp.dma_start(qs[:, k], stack_q[k].rearrange("s r h q -> (s r) h q")).then_inc(stack_in[k], 16)
                        for s in range(2):
                            sp.dma_start(kd[s * AUG:(s + 1) * AUG, k, :, s, :], stack_k[k, s]).then_inc(stack_in[k], 16)
                    if turn.runs(-2):
                        wait_apart(sp, read["OP"], turn.at(-2, 1, 1))
                        wait_apart(sp, stored, turn.at(-2, 16))
                        sp.dma_start(x_out[bass.ds(turn.at(-2, S), S), :].rearrange("(t p) d -> p t d", p=P),
                                     xo[:, turn.slot(-2)]).then_inc(stored, 16)
                    if turn.runs(0):
                        k = turn.slot(0)
                        wait_apart(sp, read["NM"], turn.at(0, 1, 1))
                        sp.dma_start(max_rows[k], nmax_t[:]).then_inc(max_out, 16)
                        wait_apart(sp, max_out, turn.at(0, 16, 16))
                        for s in range(2):
                            sp.dma_start(qs[s * AUG + ROWS:s * AUG + ROWS + 3, k], max_rows[k, 3 * H * s:3 * H * (s + 1)]
                                         .rearrange("(r h) q -> r h q", r=3)).then_inc(max_in, 16)

                turns(sp, body, -1)
                sp.wait_ge(stored, 16 * B)

            @block.gpsimd
            def _(pool):
                nc.gpsimd.memset(ident[:], 0.0)
                nc.gpsimd.memset(mask[:], 0.0)
                nc.gpsimd.memset(minus_half[:], -0.5).then_inc(setup, 1)
                pool.wait_ge(setup, 1)
                nc.gpsimd.affine_select(out=ident[:], in_=ident[:], compare_op=ALU.not_equal, fill=1.0,
                                        base=0, pattern=[[-1, P]], channel_multiplier=1)
                nc.gpsimd.affine_select(out=mask[:], in_=mask[:], compare_op=ALU.is_ge, fill=MASKED,
                                        base=0, pattern=[[0, 2], [-1, P]], channel_multiplier=1).then_inc(setup, 1)

                def ln_rstd(turn):
                    wait(pool, ln_step, turn.at(2, 3, 3))
                    nc.gpsimd.tensor_tensor(rstd[:], var_eps[:], minus_half[:], ALU.pow).then_inc(rstd_ready, 1)

                def low_part(turn, n, what):
                    if not turn.runs(1):
                        return
                    if what == "sum":
                        wait(pool, read["QK"], turn.at(1, 2, n + 1))
                        wait(pool, left_step, turn.at(0, 4, n + 1))
                        nc.gpsimd.tensor_tensor(qk[:, n], turned[:, n, 0], turned[:, n, 1], ALU.add).then_inc(qk_ready, 1)
                    elif what == "less high":
                        wait(pool, hi_ready, turn.at(1, 2, n + 1))
                        nc.gpsimd.tensor_tensor(left[:, n], qk[:, n], parts[:, n, 0], ALU.subtract).then_inc(left_step, 1)
                    else:
                        wait(pool, mid_ready, turn.at(1, 2, n + 1))
                        nc.gpsimd.tensor_tensor(parts[:, n, 2], left[:, n], parts[:, n, 1],
                                                ALU.subtract).then_inc(left_step, 1)

                def causal(turn, u):
                    wait_apart(pool, prob_ready, turn.at(-1, 12, u + 1))
                    p = prob[:, u % NP]
                    p = p.rearrange("k (a q) -> k a q", q=P) if u % 3 == 2 else \
                        p.rearrange("k (a q) -> k a q", q=S)[:, :, 0:P]
                    nc.gpsimd.affine_select(out=p, in_=p, compare_op=ALU.is_ge, fill=0.0, base=0,
                                            pattern=[[0, p.shape[1]], [1, P]], channel_multiplier=-1).then_inc(masked, 1)

                def streams(turn):
                    wait(pool, norm_step, turn.at(-2, NORM, 6))
                    ow = o_w[:].rearrange("p b (h s) d -> p (b h) s d", s=2)
                    of = o[:].rearrange("p b h d -> p (b h) d")
                    nc.gpsimd.tensor_tensor(of, ow[:, :, 0], ow[:, :, 1], ALU.add).then_inc(pool_norm, 1)
                    wait(pool, pool_norm, turn.at(-2, 5, 1))
                    of = o[:].rearrange("p b h d -> p (b h d)")
                    nc.gpsimd.tensor_tensor(o_sq[:].rearrange("p b h d -> p (b h d)"), of, of, ALU.mult).then_inc(pool_norm, 1)

                def scaled(turn):
                    wait(pool, norm_step, turn.at(-2, NORM, NORM))
                    nc.gpsimd.tensor_tensor(o_n[:].rearrange("p b h d -> p (b h) d"), o[:].rearrange("p b h d -> p (b h) d"),
                                            rrms[:].unsqueeze(2).to_broadcast([P, QB * H, HD]), ALU.mult).then_inc(pool_norm, 1)
                    wait(pool, pool_norm, turn.at(-2, 5, 3))
                    wait(pool, pe["OT"], turn.at(-3, 1, 1))
                    nc.gpsimd.tensor_tensor(o_f[:], o_n[:].rearrange("p b h d -> p b (h d)"),
                                            norm_w[:].unsqueeze(1).to_broadcast([P, QB, D]), ALU.mult).then_inc(pool_norm, 1)
                    wait(pool, xr_in[turn.slot(-2)], turn.uses(-2, 16))
                    wait(pool, read["OP"], turn.at(-3, 1, 1))
                    nc.gpsimd.tensor_tensor(xrb[:], xr[:, turn.slot(-2)], bo[:].unsqueeze(1).to_broadcast([P, QB, D]),
                                            ALU.add).then_inc(pool_norm, 1)

                pool.wait_ge(dve_setup, 6)
                pool.wait_ge(weights_in, 16 * 12)

                def body(turn):
                    for kind, u in ORDER:
                        if kind == "QK":
                            low_part(turn, u, "sum")
                        if kind == "T" and turn.runs(-1):
                            causal(turn, u)
                        if kind == "V":
                            low_part(turn, 0, "less high")
                        if kind == "NT" and u == 0:
                            low_part(turn, 1, "less high")
                        if (kind, u) == ("T", 1):
                            low_part(turn, 0, "low")
                        if (kind, u) == ("T", 2):
                            low_part(turn, 1, "low")
                            if turn.runs(-2):
                                streams(turn)
                        if (kind, u) == ("T", 6) and turn.runs(-2):
                            scaled(turn)
                        if (kind, u) == ("S", 8) and turn.runs(2):
                            ln_rstd(turn)

                ln_rstd(Turn(0, -2, False))
                turns(pool, body, -1)

            @block.scalar
            def _(act):
                act.wait_ge(dve_setup, 3)
                nc.scalar.activation(ln_ms[:], y0[:], ACT.Ln).then_inc(lam_ready, 1)
                act.wait_ge(lam_sums, 1)
                nc.scalar.activation(lam_exp[:], lam_sum[:], ACT.Exp).then_inc(lam_ready, 1)

                def body(turn):
                    for kind, u in ORDER:
                        if kind == "XT" and turn.runs(1):
                            wait_unit(act, turn, kind, u)
                            wait(act, pe["V"], turn.at(0, 1, 1))
                            nc.scalar.activation(xt[:], ring[:, 0, 0:S], ACT.Copy).then_inc(read["XT"], 1)
                        if kind == "T" and turn.runs(-1):
                            wait_unit(act, turn, kind, u)
                            wait(act, pv_done, turn.at(-1, 4, (u - NP) // 3 + 1))
                            nc.scalar.activation(prob[:, u % NP], ring[:, ORDER.index((kind, u)) % 3], ACT.Exp,
                                                 scale=SCALE).then_inc(prob_ready, 1)
                        if (kind, u) == ("QK", 1) and turn.runs(-2):
                            o_copy(turn, -2, 3)
                        if (kind, u) in (("QK", 1), ("S", 2)) and turn.runs(1):
                            n = 0 if kind == "QK" else 1
                            wait(act, qk_ready, turn.at(1, 2, n + 1))
                            wait(act, stack_out, turn.at(0, 16 * 2 * len(TERMS), 16 * 2 * len(TERMS)))
                            nc.scalar.activation(parts[:, n, 0], qk[:, n], ACT.Copy).then_inc(hi_ready, 1)
                        if (kind, u) in (("NT", 0), ("T", 0)) and turn.runs(1):
                            n = 0 if kind == "NT" else 1
                            wait(act, left_step, turn.at(1, 4, n + 1))
                            nc.scalar.activation(parts[:, n, 1], left[:, n], ACT.Copy).then_inc(mid_ready, 1)
                        if (kind, u) in (("T", 4), ("T", 7), ("T", 10)) and turn.runs(-1):
                            o_copy(turn, -1, u // 3 - 1)
                        if (kind, u) == ("T", 4) and turn.runs(-2):
                            wait(act, norm_step, turn.at(-2, NORM, 7))
                            nc.scalar.activation(ln_ms[:], ms_eps[:], ACT.Ln).then_inc(rms_step, 1)
                            wait(act, rms_step, turn.at(-2, 2, 1))
                            nc.scalar.activation(y0[:], ln_ms[:], ACT.Exp, scale=-0.5).then_inc(rms_step, 1)
                        if kind == "OT" and turn.runs(-2):
                            wait_unit(act, turn, kind, u)
                            wait(act, pe["OP"], turn.at(-3, 1, 1))
                            nc.scalar.activation(of_t[:], ring[:, ORDER.index((kind, u)) % 3, 0:S],
                                                 ACT.Copy).then_inc(read["OT"], 1)
                        if kind == "NM" and turn.runs(0):
                            wait_unit(act, turn, kind, u)
                            wait(act, max_out, turn.at(-1, 16, 16))
                            nc.scalar.activation(nmax_t[:], ring[0:2 * 3 * H, ORDER.index((kind, u)) % 3, 0:S // 2]
                                                 .bitcast(BF16), ACT.Copy).then_inc(read["NM"], 1)

                def o_copy(turn, off, g):
                    wait(act, pv_done, turn.at(off, 4, g + 1))
                    wait(act, pe["NT"], turn.at(off - 1, 2, 2))
                    nc.scalar.activation(o_t[:, g], o_ps[:, g % 2], ACT.Copy).then_inc(o_copied, 1)

                turns(act, body, -1)

            @block.vector
            def _(dve):
                nc.vector.memset(one_rows[:], 1.0).then_inc(dve_setup, 1)
                nc.vector.memset(zero_rows[:], 0.0).then_inc(dve_setup, 1)
                nc.vector.memset(y0[:], 1.0).then_inc(dve_setup, 1)
                nc.vector.memset(v[:], 0.0).then_inc(dve_setup, 1)
                nc.vector.memset(kd[:].bitcast(U32), 0).then_inc(dve_setup, 1)
                dve.wait_ge(dve_setup, 4)
                nc.vector.memset(v[:, :, :, :, HD:HD + 1], 1.0).then_inc(dve_setup, 1)
                dve.wait_ge(setup, 2)
                nc.vector.tensor_copy(ident16[:], ident[:]).then_inc(dve_setup, 1)
                dve.wait_ge(weights_in, 16 * 12)
                for n in range(2):
                    last = nc.vector.tensor_tensor(lam_prod[:, n], lam_in[:, 2 * n], lam_in[:, 2 * n + 1], ALU.mult)
                last.then_inc(lam_step, 1)
                dve.wait_ge(lam_step, 1)
                nc.vector.tensor_reduce(lam_sum[:], lam_prod[:].rearrange("p n (h d) -> p n h d", d=HD), AX.X,
                                        ALU.add).then_inc(lam_sums, 1)
                nc.vector.memset(stream_w[:, :, 0], 1.0)
                nc.vector.tensor_scalar(norm_w[:], norm_w[:], 1.0 - LAMBDA_INIT, None, ALU.mult).then_inc(lam_step, 1)
                dve.wait_ge(lam_ready, 2)
                nc.vector.scalar_tensor_tensor(out=stream_w[:, :, 1], in0=lam_exp[:, 1], scalar=-LAMBDA_INIT,
                                               in1=lam_exp[:, 0], op0=ALU.add, op1=ALU.subtract).then_inc(lam_step, 1)
                dve.wait_ge(lam_step, 3)

                def ln_stats(turn):
                    wait(dve, x_in_s[turn.slot(2)], turn.uses(2, 16))
                    for t in range(QB):
                        last = nc.vector.bn_stats(stats[:, t], x[:, turn.slot(2), t])
                    last.then_inc(ln_step, 1)
                    wait_apart(dve, ln_step, turn.at(2, 3, 1))
                    for t in range(QB):
                        last = nc.vector.bn_aggr(mean_var[:, t], stats[:, t])
                    last.then_inc(ln_step, 1)
                    wait(dve, ln_step, turn.at(2, 3, 2))
                    nc.vector.tensor_scalar(var_eps[:], mean_var[:, :, 1], LN_EPS, None, ALU.add).then_inc(ln_step, 1)

                def normalise(turn):
                    wait(dve, rstd_ready, turn.at(2, 1, 1))
                    wait(dve, pe["XT"], turn.at(1, 1, 1))
                    for t in range(QB):
                        last = nc.vector.tensor_scalar(xn[:, t], x[:, turn.slot(2), t], mean_var[:, t, 0:1],
                                                       rstd[:, t:t + 1], ALU.subtract, ALU.mult)
                    last.then_inc(xn_ready, 1)

                def body(turn):
                    def norm(instruction, n, follow=True):
                        instruction.then_inc(norm_step, 1)
                        if follow:
                            wait(dve, norm_step, turn.at(-2, NORM, n))

                    for pos, (kind, u) in enumerate(ORDER):
                        if not turn.runs(OFFSET[kind]):
                            pass
                        elif kind == "QK":
                            wait_unit(dve, turn, kind, u)
                            wait(dve, qk_ready, turn.at(0, 2, u + 1))
                            for partner in range(2):
                                for c in range(2):
                                    col = (2 * partner + c) * S
                                    n = 4 * u + 2 * partner + c
                                    last = nc.vector.scalar_tensor_tensor(
                                        out=turned[:, u, partner, c * S:(c + 1) * S], in0=ring[:, pos % 3, col:col + S],
                                        scalar=bqk[:, n:n + 1], in1=rope[:, partner], op0=ALU.add, op1=ALU.mult)
                            last.then_inc(read["QK"], 1)
                        elif kind == "V":
                            wait_unit(dve, turn, kind, u)
                            wait(dve, pv_done, turn.at(1 - NSLOT, 4, 4))
                            for t in range(QB):
                                last = nc.vector.tensor_tensor(
                                    v[:, turn.slot(1), t, :, 0:HD],
                                    ring[:, pos % 3, t * D:(t + 1) * D].rearrange("p (h d) -> p h d", d=HD),
                                    bv[:].rearrange("p (h d) -> p h d", d=HD), ALU.add)
                            last.then_inc(read["V"], 1)
                        elif kind == "S":
                            wait_unit(dve, turn, kind, u)
                            if u == 0:
                                wait(dve, max_step, turn.at(-1, 4, 4))
                            b, n, width = (0, 8 * u, P) if u < 4 else (1, 4 * (u - 4), S)
                            cnt = 1024 // width
                            nc.vector.tensor_reduce(nmax[:, b, n:n + cnt], ring[:, pos % 3]
                                                    .rearrange("p (a k) -> p a k", k=width), AX.X, ALU.max,
                                                    negate=True).then_inc(read["S"], 1)
                        elif kind == "NT":
                            wait_unit(dve, turn, kind, u)
                            got = ring[:, pos % 3].rearrange("p (a c) -> p a c", c=VW)
                            wait(dve, pool_norm, turn.at(-3, 5, 5))
                            norm(nc.vector.reciprocal(rsum[:, u], got[:, :, HD]), 3 * u + 1)
                            norm(nc.vector.tensor_tensor(rsum_w[:, u], rsum[:, u],
                                                         stream_w[:].rearrange("p h s -> p (h s)"), ALU.mult), 3 * u + 2)
                            nc.vector.tensor_tensor(o_w[:, u], got[:, :, 0:HD],
                                                    rsum_w[:, u].unsqueeze(2).to_broadcast([P, HS, HD]),
                                                    ALU.mult).then_inc(norm_step, 1)
                        elif kind == "OP":
                            wait_unit(dve, turn, kind, u)
                            wait(dve, pool_norm, turn.at(-2, 5, 5))
                            wait(dve, stored, turn.at(-3, 16, 16))
                            nc.vector.tensor_tensor(xo[:, turn.slot(-2)], ring[:, pos % 3, 0:S]
                                                    .rearrange("p (t d) -> p t d", d=D), xrb[:], ALU.add).then_inc(read["OP"], 1)
                        if (kind, u) == ("S", 6) and turn.runs(-2):
                            wait(dve, pool_norm, turn.at(-2, 5, 2))
                            nc.vector.tensor_reduce(ms[:], o_sq[:].rearrange("p b h d -> p (b h) d"), AX.X,
                                                    ALU.add).then_inc(ms_ready, 1)
                            wait(dve, ms_ready, turn.at(-2, 1, 1))
                            norm(nc.vector.tensor_scalar(ms_eps[:], ms[:], 1.0 / HD, RMS_EPS, ALU.mult, ALU.add), 7, False)
                        if (kind, u) == ("S", 8) and turn.runs(-2):
                            wait(dve, rms_step, turn.at(-2, 2, 2))
                            norm(nc.vector.tensor_tensor(newton[:], ms_eps[:], y0[:], ALU.mult), 8)
                            norm(nc.vector.tensor_tensor(newton2[:], newton[:], y0[:], ALU.mult), 9)
                            norm(nc.vector.tensor_scalar(newton[:], newton2[:], -0.5, 1.5, ALU.mult, ALU.add), 10)
                            norm(nc.vector.tensor_tensor(rrms[:], newton[:], y0[:], ALU.mult), 11, False)
                        if (kind, u) == ("S", 7) and turn.runs(2):
                            ln_stats(turn)
                        if (kind, u) == ("S", 10) and turn.runs(2):
                            normalise(turn)
                        if (kind, u) == ("S", 11) and turn.runs(0):
                            def part(instruction, n):
                                instruction.then_inc(max_step, 1)
                                wait(dve, max_step, turn.at(0, 4, n))

                            def rows(n):
                                return nmax_parts[:, :, :, n].rearrange("p b s h -> p b h s")

                            def flat(t):
                                return t[:].rearrange("p b (h s) -> p b h s", s=2)

                            wait(dve, read["S"], turn.at(0, 12, 12))
                            wait(dve, pe["NM"], turn.at(-1, 1, 1))
                            part(nc.vector.tensor_copy(rows(0), flat(nmax)), 1)
                            part(nc.vector.tensor_tensor(flat(nmax_left), flat(nmax), rows(0), ALU.subtract), 2)
                            part(nc.vector.tensor_copy(rows(1), flat(nmax_left)), 3)
                            nc.vector.tensor_tensor(rows(2), flat(nmax_left), rows(1), ALU.subtract).then_inc(max_step, 1)

                first = Turn(0, -2, False)
                ln_stats(first)
                normalise(first)
                turns(dve, body, -1)

            @block.tensor
            def _(te):
                te.wait_ge(dve_setup, 7)
                te.wait_ge(weights_in, 16 * 12)

                def free(turn, pos):
                    back = pos - 3
                    c = turn.c
                    while True:
                        if back < 0:
                            back, c = back + len(ORDER), c - 1
                        if not turn.looped and c < -1:
                            return
                        kind, u = ORDER[back]
                        before = Turn(turn.r, c, turn.looped)
                        if before.runs(OFFSET[kind]):
                            break
                        back -= 3
                    if kind == "T":
                        wait(te, prob_ready, before.at(OFFSET[kind], 12, u + 1))
                    elif kind == "NT":
                        wait(te, norm_step, before.at(OFFSET[kind], NORM, 3 * u + 3))
                    else:
                        wait(te, read[kind], before.at(OFFSET[kind], UNITS[kind], u + 1))

                def mm(out, lhs, rhs, start=True, stop=True):
                    return nc.tensor.matmul(out, lhs, rhs, start=start, stop=stop)

                def weigh(turn, off, g):
                    wait(te, masked, turn.at(off, 12, 3 * g + 3))
                    wait(te, o_copied, turn.at(off, 4, g - 1))
                    k = turn.slot(off)
                    for j in range(2):
                        for b in range(2):
                            for i in range(4):
                                h = (8 * g + 4 * j + i) // 2
                                p = prob[:, (3 * g + j) % NP, i * S:(i + 1) * S] if b == 0 else \
                                    prob[:, (3 * g + 2) % NP, (4 * j + i) * P:(4 * j + i + 1) * P]
                                last = nc.tensor.matmul(o_ps[VW * i:VW * (i + 1), g % 2, j, b * P:S], v[:, k, b, h], p,
                                                        start=(b == 0), stop=(b == 1), tile_position=(0, VW * i))
                    last.then_inc(pv_done, 1)

                def body(turn):
                    for pos, (kind, u) in enumerate(ORDER):
                        buf = ring[:, pos % 3]
                        if turn.runs(OFFSET[kind]):
                            free(turn, pos)
                            if kind == "XT":
                                wait(te, xn_ready, turn.at(1, 1, 1))
                                for t in range(QB):
                                    last = nc.tensor.transpose(buf[:, t * P:(t + 1) * P], xn[:, t], ident[:])
                            elif kind == "QK":
                                wait(te, read["XT"], turn.at(1, 1, 1))
                                for n in range(4):
                                    last = mm(buf[:, n * S:(n + 1) * S], wqk[:, 4 * u + n], xt[:])
                            elif kind == "V":
                                for t in range(QB):
                                    last = mm(buf[:, t * D:(t + 1) * D], xt[:, t * P:(t + 1) * P], wv[:])
                            elif kind == "S":
                                k = turn.slot(0)
                                if u == 0:
                                    wait(te, stack_in[k], turn.uses(0, 48))
                                b, h0, width = (0, 4 * u, P) if u < 4 else (1, 2 * (u - 4), S)
                                for n in range(1024 // (2 * width)):
                                    out = buf[:, n * 2 * width:(n + 1) * 2 * width].rearrange("q (s k) -> q s k", s=2)
                                    mm(out, qs[:, k, h0 + n, b * P:(b + 1) * P], kd[:, k, h0 + n, :, 0:width], stop=False)
                                    last = mm(out[:, :, b * P:(b + 1) * P], ident16[:], mask[:], start=False)
                            elif kind == "T":
                                k = turn.slot(-1)
                                if u == 0:
                                    wait(te, max_in, turn.at(-1, 32, 32))
                                g, n = divmod(u, 3)
                                for i in range(8 if n == 2 else 4):
                                    hs = 8 * g + (i if n == 2 else 4 * n + i)
                                    b = 1 if n == 2 else 0
                                    q0 = b * P
                                    last = mm(buf[:, i * (S - q0):(i + 1) * (S - q0)],
                                              kd[:, k, hs // 2, hs % 2, b * P:(b + 1) * P], qs[:, k, hs // 2, q0:S])
                            elif kind == "NT":
                                wait(te, o_copied, turn.at(-2, 4, 4))
                                for n in range(8):
                                    last = nc.tensor.transpose(buf[:, n * P:(n + 1) * P],
                                                               o_t[:, n // 2, n % 2, u * P:(u + 1) * P], ident[:])
                            elif kind == "OT":
                                wait(te, pool_norm, turn.at(-2, 5, 4))
                                for t in range(QB):
                                    last = nc.tensor.transpose(buf[:, t * P:(t + 1) * P], o_f[:, t], ident[:])
                            elif kind == "OP":
                                wait(te, read["OT"], turn.at(-2, 1, 1))
                                for t in range(QB):
                                    last = mm(buf[:, t * D:(t + 1) * D], of_t[:, t * P:(t + 1) * P], wo[:])
                            elif kind == "NM":
                                wait(te, max_step, turn.at(0, 4, 4))
                                for b in range(QB):
                                    last = nc.tensor.transpose(
                                        buf[0:2 * 3 * H, b * P // 2:(b + 1) * P // 2].bitcast(BF16),
                                        nmax_parts[:, b].rearrange("p s r h -> p (s r h)"), ident16[:])
                            last.then_inc(pe[kind], 1)
                        if (kind, u) == ("S", 0) and turn.runs(-2):
                            weigh(turn, -2, 3)
                        if (kind, u) in (("T", 4), ("T", 7), ("T", 10)) and turn.runs(-1):
                            weigh(turn, -1, u // 3 - 1)

                turns(te, body, -1)


def layout(L0_attn_x, L0_attn_Wq, L0_attn_bq, L0_attn_Wk, L0_attn_bk, L0_attn_Wv, L0_attn_bv, L0_attn_Wo, L0_attn_bo,
           L0_attn_head_norm_w, L0_attn_lq1, L0_attn_lk1, L0_attn_lq2, L0_attn_lk2, L0_ffn_gate_w,
           L0_ffn_balance_bias, L0_ffn_w1, L0_ffn_w2):
    c = np.ascontiguousarray
    order = np.array([[[[(2 * pp + ch) * 2 * HD + s * HD + d for pp in range(H // 2)] for d in range(HD)]
                       for s in range(2)] for ch in range(2)]).reshape(2, P)
    partner = np.where(order % HD < HD // 2, order + HD // 2, order - HD // 2)
    rows = np.stack([order, partner])
    wqk = np.stack([L0_attn_Wq[rows], L0_attn_Wk[rows]])
    bqk = np.stack([L0_attn_bq[rows], L0_attn_bk[rows]])
    half = HD // 2
    freq = np.float32(1.0) / np.power(np.float32(10000.0), np.arange(half, dtype=np.float32) / np.float32(half))
    angle = (np.arange(S, dtype=np.float32)[None, :] * freq[:, None]).astype(np.float64)
    d = order[0] % HD
    cos = np.cos(angle)[d % half]
    sin = np.sin(angle)[d % half] * np.where(d < half, -1.0, 1.0)[:, None]
    return {
        "x": c(L0_attn_x.reshape(T, D)),
        "gate_w": c(L0_ffn_gate_w.T),
        "gate_b": c(L0_ffn_balance_bias),
        "w1": c(L0_ffn_w1.reshape(E * EH, D).T),
        "w2": c(L0_ffn_w2.transpose(0, 2, 1).reshape(HC, P, D).transpose(1, 0, 2)),
        "wqk": c(wqk.reshape(2 * NC4, P, D).transpose(2, 0, 1)),
        "bqk": c(bqk.reshape(2 * NC4, P).T),
        "wv": c(L0_attn_Wv.T),
        "wo": c(L0_attn_Wo.T),
        "bv": c(L0_attn_bv),
        "bo": c(L0_attn_bo),
        "norm_w": c(L0_attn_head_norm_w.reshape(D)),
        "lq1": c(L0_attn_lq1.reshape(D)), "lk1": c(L0_attn_lk1.reshape(D)),
        "lq2": c(L0_attn_lq2.reshape(D)), "lk2": c(L0_attn_lk2.reshape(D)),
        "rope": c(np.stack([cos, sin], 1).astype(np.float32)),
    }


def build(nc, a, out):
    x1 = nc.dram_tensor("x1", (T, D), F32).ap()
    x2 = nc.dram_tensor("x2", (T, D), F32).ap()
    ffn(nc, "ffn1", a["x"], x1, a)
    attention(nc, "att", x1, x2, a)
    ffn(nc, "ffn2", x2, out, a)



def kernel(**inputs):
    import numpy as _np
    import concourse.bacc as _bacc
    from concourse.bass_utils import run_bass_kernel_spmd as _run

    arrays = layout(**{k: _np.asarray(v) for k, v in inputs.items()})
    nc = _bacc.Bacc("TRN2", target_bir_lowering=False, num_devices=1)
    aps = {n: nc.dram_tensor(n, a.shape, mybir.dt.from_np(a.dtype), kind="ExternalInput").ap()
           for n, a in arrays.items()}
    out = nc.dram_tensor("out", (T, D), F32, kind="ExternalOutput").ap()
    build(nc, aps, out)
    r = _run(nc, [arrays], core_ids=[0])
    return r.results[0]["out"].reshape(B, S, D)
```

```python
import math
from contextlib import ExitStack

import numpy as np

import concourse.bass as bass
from concourse import mybir

F32 = mybir.dt.float32
F32R = mybir.dt.float32r
BF16 = mybir.dt.bfloat16
U32 = mybir.dt.uint32
ALU = mybir.AluOpType
ACT = mybir.ActivationFunctionType
AX = mybir.AxisListType

P = 128
D = 128
B, S = 32, 256
T = B * S
H, HD = 16, 8
HS = 2 * H
LAMBDA_INIT = 0.8 - 0.6 * math.exp(-0.3 * 0)
RMS_EPS = 1e-6
LN_EPS = 1e-5
SCALE = 1.0 / math.sqrt(HD)
E, EH = 8, 256
MASKED = -1e30


def wait(engine, semaphore, count):
    if isinstance(count, int) and count <= 0:
        return
    engine.wait_ge(semaphore, count)


def wait_apart(engine, semaphore, count):
    wait(engine, semaphore, count)
    engine.nop(nofuse=True)



FT = 512
FB = T // FT
FTT = FT // P
HC = E * EH // P
HE = EH // P
NX = 3
NH = 4
NUP = 2
SCALE_LAG, LOW_LAG, DOWN_LAG = 1, 2, 3
POOL_LOW = (3, 4, 5, 6, 7)
PRODUCTS = ((0, 0), (0, 1), (1, 0))
LOW_ROW = 32


class Block:

    def __init__(self, r, c, looped):
        self.r, self.c, self.looped = r, c, looped

    def exists(self):
        return self.looped or 0 <= self.c < FB

    def at(self, per=1, add=0):
        return self.r * (NX * per) + (self.c * per + add)

    def slot(self):
        return self.c % NX

    def uses(self, per=1):
        return self.r * per + (self.c // NX + 1) * per

    def shift(self, n):
        return Block(self.r, self.c + n, self.looped)

    def behind(self, e, lag):
        return (self, e - lag) if e >= lag else (self.shift(-1), e - lag + E)


def blocks(engine, body):
    start = NX
    for j in range(-2, start):
        body(Block(0, j, False))
    n = (FB - 2 - start) // NX
    with engine.Fori(0, n) as r:
        for k in range(NX):
            body(Block(r, start + k, True))
    for j in range(start + NX * n, FB + 1):
        body(Block(0, j, False))


def ffn(nc, tag, x_in, x_out, w):
    with ExitStack() as ctx:
        def sb(name, shape, dt=F32):
            return ctx.enter_context(nc.sbuf_tensor(f"{tag}_{name}", shape, dt))

        def ps(name, shape, dt=F32):
            return ctx.enter_context(nc.psum_tensor(f"{tag}_{name}", shape, dt))

        def sem(name):
            return ctx.enter_context(nc.semaphore(f"{tag}_{name}"))

        w1 = sb("w1", [P, E * EH])
        w2 = sb("w2", [P, HC * D])
        gate_w = sb("gate_w", [P, E])
        w1s = [sb(f"w1_{n}", [P, E * EH], F32R) for n in ("high", "low")]
        w2s = [sb(f"w2_{n}", [P, HC * D], F32R) for n in ("high", "low")]
        gate_ws = [sb(f"gate_w_{n}", [P, E], F32R) for n in ("high", "low")]
        gate_b = sb("gate_b", [P, E])
        ident = sb("ident", [P, P])
        zeros = sb("zeros", [P, FT])
        one_at = sb("one_at", [P, E, P])
        expert_rows = sb("expert_rows", [P, E, P], F32R)
        iota = sb("iota", [P, E])
        e_const = sb("e_const", [P, FTT * E])
        minus_half = sb("minus_half", [P, FTT])
        x = sb("x", [P, NX, FTT, D])
        stats = sb("stats", [P, FTT, 6])
        mean_var = sb("mean_var", [P, FTT, 2])
        var_eps = sb("var_eps", [P, FTT])
        rstd = sb("rstd", [P, FTT])
        xn = sb("xn", [P, FTT, D])
        xts = [sb(f"xt_{n}", [P, NX, FT], F32R) for n in ("high", "low")]
        nz = sb("nz", [P, FTT, E])
        ez = sb("ez", [P, FTT, E])
        score = sb("score", [P, FTT, E])
        rest = sb("rest", [P, FTT, E])
        pick1 = sb("pick1", [P, FTT, E])
        pick2 = sb("pick2", [P, FTT, E])
        picked = sb("picked", [P, FTT, E])
        top = sb("top", [P, 2, FTT, 8])
        top_at = sb("top_at", [P, 2, FTT, 8], U32)
        top_atf = sb("top_atf", [P, 2, FTT])
        denom = sb("denom", [P, FTT])
        rdenom = sb("rdenom", [P, FTT])
        comb = sb("comb", [P, FTT, E])
        comb_rows = sb("comb_rows", [P, NX, FT], F32R)
        h = sb("h", [P, NH, HE, FT])
        hts = [sb(f"h_{n}", [P, NH, HE, FT], F32R) for n in ("high", "low")]
        y_sb = sb("y_sb", [P, FT])
        out = sb("out", [P, NX, FTT, D])

        up = ps("up", [P, NUP, HE, FT])
        y = ps("y", [P, FT])
        weight_ps = ps("weight_ps", [P, FT])
        turn_ps = ps("turn_ps", [P, FT])
        gate_ps = ps("gate_ps", [P, FT])

        weights_in = sem("weights_in")
        const_step = sem("const_step")
        rows_set = sem("rows_set")
        x_in_s = [sem(f"x_in{k}") for k in range(NX)]
        stored = sem("stored")
        ln_step = sem("ln_step")
        rstd_ready = sem("rstd_ready")
        xn_ready = sem("xn_ready")
        transposed = sem("transposed")
        xt_high = sem("xt_high")
        xt_ready = sem("xt_ready")
        logits_done = sem("logits_done")
        z_ready = sem("z_ready")
        ez_ready = sem("ez_ready")
        gate_step = sem("gate_step")
        comb_ready = sem("comb_ready")
        comb_turned = sem("comb_turned")
        rows_high = sem("rows_high")
        rows_ready = sem("rows_ready")
        up_done = sem("up_done")
        silu_ready = sem("silu_ready")
        weight_done = sem("weight_done")
        scaled = sem("scaled")
        high_ready = sem("high_ready")
        expert_done = sem("expert_done")
        low_by_pool = sem("low_by_pool")
        low_by_dve = sem("low_by_dve")
        y_copied = sem("y_copied")
        y_turned = sem("y_turned")
        added = sem("added")
        split_high = sem("split_high")
        split_low = sem("split_low")

        LN, GATE = 3, 13
        ON_DVE = E - len(POOL_LOW)

        def wait_low(engine, b, e):
            if e < 0:
                b, e = b.shift(-1), e + E
            before = sum(p < e for p in POOL_LOW)
            if e in POOL_LOW:
                wait(engine, low_by_pool, b.at(len(POOL_LOW), before + 1))
            else:
                wait(engine, low_by_dve, b.at(ON_DVE, e - before + 1))

        weights = ((gate_w, gate_ws), (w1, w1s), (w2, w2s))

        with nc.Block() as block:

            @block.sync
            def _(sp):
                def load_x(b):
                    sp.dma_start(x[:, b.slot()], x_in[bass.ds(b.at(FT), FT), :].rearrange("(t p) d -> p t d", p=P)
                                 ).then_inc(x_in_s[b.slot()], 16)

                load_x(Block(0, 0, False))
                load_x(Block(0, 1, False))
                for name, dst in (("gate_w", gate_w), ("w1", w1), ("w2", w2)):
                    sp.dma_start(dst[:], w[name]).then_inc(weights_in, 16)
                sp.dma_start(gate_b[:], w["gate_b"].partition_broadcast(P)).then_inc(weights_in, 16)

                def body(b):
                    if b.shift(-1).exists():
                        wait_apart(sp, added, b.at())
                        wait_apart(sp, stored, b.shift(-1).at(16))
                        sp.dma_start(x_out[bass.ds(b.shift(-1).at(FT), FT), :].rearrange("(t p) d -> p t d", p=P),
                                     out[:, b.shift(-1).slot()]).then_inc(stored, 16)
                    if b.shift(2).exists() and (b.looped or b.c >= 0):
                        load_x(b.shift(2))

                blocks(sp, body)
                sp.wait_ge(stored, 16 * FB)

            @block.gpsimd
            def _(pool):
                nc.gpsimd.memset(ident[:], 0.0)
                nc.gpsimd.memset(zeros[:], 0.0)
                nc.gpsimd.memset(one_at[:], 0.0)
                nc.gpsimd.memset(e_const[:], math.e)
                nc.gpsimd.memset(minus_half[:], -0.5)
                nc.gpsimd.iota(iota[:], pattern=[[1, E]], base=0, channel_multiplier=0,
                               allow_small_or_imprecise_dtypes=True).then_inc(const_step, 1)
                pool.wait_ge(const_step, 1)
                nc.gpsimd.affine_select(out=ident[:], in_=ident[:], compare_op=ALU.not_equal, fill=1.0,
                                        base=0, pattern=[[-1, P]], channel_multiplier=1).then_inc(const_step, 1)
                for n, row in enumerate((0, LOW_ROW)):
                    nc.gpsimd.affine_select(out=one_at[:], in_=one_at[:], compare_op=ALU.not_equal, fill=1.0,
                                            base=-row, pattern=[[-1, E], [0, P]], channel_multiplier=1
                                            ).then_inc(const_step, 1)
                    pool.wait_ge(const_step, 3 + n)

                def ln_rstd(b):
                    wait(pool, ln_step, b.at(LN, 3))
                    nc.gpsimd.tensor_tensor(rstd[:], var_eps[:], minus_half[:], ALU.pow).then_inc(rstd_ready, 1)

                def gate_exp(b, part):
                    wait(pool, z_ready, b.at(1, 1))
                    k = slice(part * FTT // 2, (part + 1) * FTT // 2)
                    n = FTT * E // 2
                    nc.gpsimd.tensor_tensor(ez[:, k].rearrange("p t e -> p (t e)"), e_const[:, 0:n],
                                            nz[:, k].rearrange("p t e -> p (t e)"), ALU.pow).then_inc(ez_ready, 1)

                def low(b, e):
                    if b.exists() and e in POOL_LOW:
                        wait(pool, high_ready, b.at(E, e + 1))
                        wait(pool, expert_done, b.at(E, e - NH + 1))
                        nc.gpsimd.tensor_tensor(hts[1][:, e % NH], h[:, e % NH], hts[0][:, e % NH],
                                                ALU.subtract).then_inc(low_by_pool, 1)

                def body(b):
                    ahead = b.shift(1)
                    for e in range(E):
                        low(*b.behind(e, LOW_LAG))
                        if ahead.exists() and e in (3, 4):
                            gate_exp(ahead, e - 3)
                        if b.shift(2).exists() and e == 6:
                            ln_rstd(b.shift(2))

                blocks(pool, body)

            @block.scalar
            def _(act):
                def weight_high(n):
                    nc.scalar.activation(weights[n][1][0][:], weights[n][0][:], ACT.Copy).then_inc(split_high, 1)

                act.wait_ge(const_step, 4)
                nc.scalar.activation(expert_rows[:], one_at[:], ACT.Copy)
                for k in range(NX):
                    last = nc.scalar.activation(comb_rows[:, k], zeros[:], ACT.Copy)
                last.then_inc(rows_set, 1)
                act.wait_ge(rows_set, 1)

                def xt_copy(b):
                    wait(act, transposed, b.at(1, 1))
                    nc.scalar.activation(xts[0][:, b.slot()], turn_ps[:], ACT.Copy).then_inc(xt_high, 1)

                def rows_copy(b):
                    wait(act, comb_turned, b.at(1, 1))
                    nc.scalar.activation(comb_rows[0:E, b.slot()], gate_ps[0:E, :], ACT.Copy).then_inc(rows_high, 1)

                def silu(b, e):
                    if b.exists():
                        wait(act, up_done, b.at(E, e + 1))
                        wait_low(act, b, e - NH)
                        nc.scalar.activation(h[:, e % NH], up[:, e % NUP], ACT.Silu).then_inc(silu_ready, 1)

                def high(b, e):
                    if b.exists():
                        wait(act, scaled, b.at(E, e + 1))
                        wait(act, expert_done, b.at(E, e - NH + 1))
                        nc.scalar.activation(hts[0][:, e % NH], h[:, e % NH], ACT.Copy).then_inc(high_ready, 1)

                def copy_y(b):
                    wait(act, expert_done, b.at(E, E))
                    wait(act, y_turned, b.at())
                    nc.scalar.activation(y_sb[:], y[:], ACT.Copy).then_inc(y_copied, 1)

                def body(b):
                    ahead = b.shift(1)
                    if b.c == -1:
                        act.wait_ge(weights_in, 64)
                        weight_high(0)
                    for e in range(E):
                        silu(b, e)
                        if e == 0 and ahead.exists():
                            xt_copy(ahead)
                        if e == 0 and b.exists():
                            rows_copy(b)
                        high(*b.behind(e, SCALE_LAG))
                        if e == 1 and b.c == -1:
                            weight_high(1)
                            weight_high(2)
                        if e == 2 and b.shift(-1).exists():
                            copy_y(b.shift(-1))

                blocks(act, body)

            @block.vector
            def _(dve):
                def ln_stats(b):
                    wait(dve, x_in_s[b.slot()], b.uses(16))
                    for t in range(FTT):
                        last = nc.vector.bn_stats(stats[:, t], x[:, b.slot(), t])
                    last.then_inc(ln_step, 1)
                    wait_apart(dve, ln_step, b.at(LN, 1))
                    for t in range(FTT):
                        last = nc.vector.bn_aggr(mean_var[:, t], stats[:, t])
                    last.then_inc(ln_step, 1)
                    wait(dve, ln_step, b.at(LN, 2))
                    nc.vector.tensor_scalar(var_eps[:], mean_var[:, :, 1], LN_EPS, None, ALU.add).then_inc(ln_step, 1)

                def normalise(b):
                    wait(dve, rstd_ready, b.at(1, 1))
                    wait(dve, transposed, b.at())
                    for t in range(FTT):
                        last = nc.vector.tensor_scalar(xn[:, t], x[:, b.slot(), t], mean_var[:, t, 0:1],
                                                       rstd[:, t:t + 1], ALU.subtract, ALU.mult)
                    last.then_inc(xn_ready, 1)

                def xt_low(b):
                    wait(dve, xt_high, b.at(1, 1))
                    nc.vector.tensor_tensor(xts[1][:, b.slot()], turn_ps[:], xts[0][:, b.slot()],
                                            ALU.subtract).then_inc(xt_ready, 1)

                def logits(b):
                    wait(dve, logits_done, b.at(1, 1))
                    nc.vector.scalar_tensor_tensor(out=nz[:], in0=gate_ps[:, 0:FTT * E].rearrange("p (t e) -> p t e", e=E),
                                                   scalar=-1.0, in1=gate_b[:].unsqueeze(1).to_broadcast([P, FTT, E]),
                                                   op0=ALU.mult, op1=ALU.subtract).then_inc(z_ready, 1)

                def gate(b, part):

                    def round_of(n, *operations):
                        wait_apart(dve, gate_step, b.at(GATE, n))
                        for operation in operations:
                            last = operation()
                        last.then_inc(gate_step, 1)

                    def best(n, scores):
                        def f():
                            for t in range(FTT):
                                last = nc.vector.max(top[:, n, t], scores[:, t])
                            return last
                        return f

                    def best_at(n, scores):
                        def f():
                            for t in range(FTT):
                                last = nc.vector.max_index(top_at[:, n, t], top[:, n, t], scores[:, t])
                            return last
                        return f

                    def as_float(n):
                        return lambda: nc.vector.tensor_copy(top_atf[:, n], top_at[:, n, :, 0])

                    def mark(n, to):
                        return lambda: nc.vector.tensor_tensor(
                            to[:], iota[:].unsqueeze(1).to_broadcast([P, FTT, E]),
                            top_atf[:, n].unsqueeze(2).to_broadcast([P, FTT, E]), ALU.is_equal)

                    if part == 0:
                        wait(dve, ez_ready, b.at(2, 2))
                        round_of(0, lambda: nc.vector.tensor_scalar(rest[:], ez[:], 1.0, None, ALU.add))
                        round_of(1, lambda: nc.vector.reciprocal(score[:], rest[:]))
                    elif part == 1:
                        round_of(2, best(0, score))
                        round_of(3, best_at(0, score))
                    elif part == 2:
                        round_of(4, as_float(0))
                        round_of(5, mark(0, pick1))
                    elif part == 3:
                        round_of(6, lambda: nc.vector.scalar_tensor_tensor(
                            out=rest[:], in0=pick1[:], scalar=-2.0, in1=score[:], op0=ALU.mult, op1=ALU.add))
                        round_of(7, best(1, rest))
                    elif part == 4:
                        round_of(8, best_at(1, rest),
                                 lambda: nc.vector.tensor_tensor(denom[:], top[:, 0, :, 0], top[:, 1, :, 0], ALU.add))
                        round_of(9, as_float(1),
                                 lambda: nc.vector.tensor_scalar(denom[:], denom[:], 1e-6, 2.0, ALU.add, ALU.mult))
                    elif part == 5:
                        round_of(10, mark(1, pick2), lambda: nc.vector.reciprocal(rdenom[:], denom[:]))
                        round_of(11, lambda: nc.vector.tensor_tensor(picked[:], pick1[:], pick2[:], ALU.add))
                    else:
                        round_of(12, lambda: nc.vector.tensor_tensor(picked[:], picked[:], score[:], ALU.mult))
                        wait(dve, gate_step, b.at(GATE, GATE))
                        wait(dve, comb_turned, b.at())
                        nc.vector.tensor_tensor(comb[:], picked[:], rdenom[:].unsqueeze(2).to_broadcast([P, FTT, E]),
                                                ALU.mult).then_inc(comb_ready, 1)

                def rows_low(b):
                    wait(dve, rows_high, b.at(1, 1))
                    nc.vector.tensor_tensor(comb_rows[LOW_ROW:LOW_ROW + E, b.slot()], gate_ps[0:E, :],
                                            comb_rows[0:E, b.slot()], ALU.subtract).then_inc(rows_ready, 1)

                def scale(b, e):
                    if b.exists():
                        wait(dve, silu_ready, b.at(E, e + 1))
                        wait(dve, weight_done, b.at(E, e + 1))
                        nc.vector.tensor_tensor(h[:, e % NH], h[:, e % NH],
                                                weight_ps[:].unsqueeze(1).to_broadcast([P, HE, FT]),
                                                ALU.mult).then_inc(scaled, 1)

                def low(b, e):
                    if b.exists() and e not in POOL_LOW:
                        wait(dve, high_ready, b.at(E, e + 1))
                        nc.vector.tensor_tensor(hts[1][:, e % NH], h[:, e % NH], hts[0][:, e % NH],
                                                ALU.subtract).then_inc(low_by_dve, 1)

                def add_x(b):
                    wait(dve, y_turned, b.at(1, 1))
                    wait(dve, stored, b.shift(-1).at(16))
                    nc.vector.tensor_tensor(out[:, b.slot()], turn_ps[:].rearrange("p (t d) -> p t d", t=FTT),
                                            x[:, b.slot()], ALU.add).then_inc(added, 1)

                def weight_low(n):
                    dve.wait_ge(split_high, n + 1)
                    nc.vector.tensor_tensor(weights[n][1][1][:], weights[n][0][:], weights[n][1][0][:],
                                            ALU.subtract).then_inc(split_low, 1)

                dve.wait_ge(rows_set, 1)

                def body(b):
                    ahead = b.shift(1)
                    for e in range(E):
                        if e == 0 and b.exists():
                            gate(b, 6)
                        scale(*b.behind(e, SCALE_LAG))
                        if e >= 5 and ahead.exists():
                            gate(ahead, 2 * (e - 5))
                        low(*b.behind(e, LOW_LAG))
                        if e == 4 and b.shift(-1).exists():
                            add_x(b.shift(-1))
                        if e == (4 if b.c == -1 else 6) and b.shift(2).exists():
                            ln_stats(b.shift(2))
                        if e == 7 and b.shift(2).exists():
                            normalise(b.shift(2))
                        if e >= 5 and ahead.exists():
                            gate(ahead, 2 * (e - 5) + 1)
                        if e == 0 and b.exists():
                            rows_low(b)
                        if e == 1 and ahead.exists():
                            if b.c == -1:
                                weight_low(0)
                            xt_low(ahead)
                        if e == 2 and ahead.exists():
                            logits(ahead)
                            if b.c == -1:
                                weight_low(1)
                                weight_low(2)

                blocks(dve, body)

            @block.tensor
            def _(pe):
                def transpose_x(b):
                    wait(pe, xn_ready, b.at(1, 1))
                    wait(pe, added, b.shift(-2).at())
                    for t in range(FTT):
                        last = nc.tensor.transpose(turn_ps[:, t * P:(t + 1) * P], xn[:, t], ident[:])
                    last.then_inc(transposed, 1)

                def gate_logits(b):
                    wait(pe, xt_ready, b.at(1, 1))
                    wait(pe, rows_ready, b.at())
                    for t in range(FTT):
                        for n in range(4):
                            last = nc.tensor.matmul(gate_ps[:, t * E:(t + 1) * E], xts[n // 2][:, b.slot(), t * P:(t + 1) * P],
                                                    gate_ws[n % 2][:], start=(n == 0), stop=(n == 3))
                    last.then_inc(logits_done, 1)

                def transpose_comb(b):
                    wait(pe, comb_ready, b.at(1, 1))
                    for t in range(FTT):
                        last = nc.tensor.transpose(gate_ps[0:E, t * P:(t + 1) * P], comb[:, t], ident[:])
                    last.then_inc(comb_turned, 1)

                def up_product(b, e):
                    if b.exists():
                        wait(pe, silu_ready, b.at(E, e - NUP + 1))
                        for k in range(HE):
                            col = (HE * e + k) * P
                            for n, (a1, a2) in enumerate(PRODUCTS):
                                last = nc.tensor.matmul(up[:, e % NUP, k], w1s[a1][:, col:col + P], xts[a2][:, b.slot()],
                                                        start=(n == 0), stop=(n == 2))
                        last.then_inc(up_done, 1)

                def spread_weight(b, e):
                    if b.exists():
                        wait(pe, scaled, b.at(E, e))
                        if e == 0:
                            wait(pe, rows_ready, b.at(1, 1))
                        nc.tensor.matmul(weight_ps[:], expert_rows[:, e], comb_rows[:, b.slot()],
                                         start=True, stop=True).then_inc(weight_done, 1)

                def down_product(b, e):
                    if b.exists():
                        wait_low(pe, b, e)
                        if e == 0:
                            wait(pe, y_copied, b.at())
                        for k in range(HE):
                            col = (HE * e + k) * D
                            for n, (a1, a2) in enumerate(PRODUCTS):
                                last = nc.tensor.matmul(y[:], w2s[a1][:, col:col + D], hts[a2][:, e % NH, k],
                                                        start=(e == 0 and k == 0 and n == 0),
                                                        stop=(e == E - 1 and k == HE - 1 and n == 2))
                        last.then_inc(expert_done, 1)

                def transpose_y(b):
                    wait(pe, y_copied, b.at(1, 1))
                    if b.shift(2).exists():
                        wait(pe, xt_ready, b.shift(2).at(1, 1))
                    for t in range(FTT):
                        last = nc.tensor.transpose(turn_ps[:, t * P:(t + 1) * P], y_sb[:, t * P:(t + 1) * P], ident[:])
                    last.then_inc(y_turned, 1)

                pe.wait_ge(const_step, 2)

                def body(b):
                    ahead = b.shift(1)
                    for e in range(E):
                        if b.c == 0 and e == 0:
                            pe.wait_ge(split_low, 3)
                        if e == 2 and ahead.exists():
                            if b.c == -1:
                                pe.wait_ge(split_low, 1)
                            gate_logits(ahead)
                        spread_weight(*b.behind(e, SCALE_LAG))
                        up_product(b, e)
                        if e == 0 and ahead.exists():
                            transpose_x(ahead)
                        if e == 0 and b.exists():
                            transpose_comb(b)
                        down_product(*b.behind(e, DOWN_LAG))
                        if e == 3 and b.shift(-1).exists():
                            transpose_y(b.shift(-1))

                blocks(pe, body)



NSLOT = 3
NP = 12
TERMS = ((0, 0), (0, 1), (0, 2), (1, 0), (1, 1), (2, 0))
ROWS = len(TERMS) * HD
AUG = 52
QB = S // P
NC4 = 4
VW = 32

ORDER = [("XT", 0), ("T", 6), ("QK", 0), ("NM", 0), ("QK", 1), ("S", 0), ("S", 1), ("T", 7), ("T", 8), ("S", 2),
         ("S", 3), ("T", 9), ("S", 4), ("T", 10), ("S", 5), ("T", 11), ("S", 6), ("S", 7), ("T", 0), ("V", 0),
         ("T", 1), ("T", 2), ("NT", 0), ("NT", 1), ("OT", 0), ("S", 8), ("OP", 0), ("S", 9), ("T", 3), ("S", 10),
         ("T", 4), ("S", 11), ("T", 5)]
AFTER = {
    "rotate 0": ("T", 6), "rotate 1": ("T", 7),
    "left 0": ("T", 8), "left 1": ("T", 9), "low 0": ("T", 10), "low 1": ("T", 0),
    "high 0": ("QK", 1), "high 1": ("T", 8), "mid 0": ("T", 9), "mid 1": ("T", 10),
    "weigh 0": ("T", 5), "weigh 1": ("T", 7), "weigh 2": ("T", 11), "weigh 3": ("T", 0),
    "copy 0": ("T", 5), "copy 1": ("T", 7), "copy 2": ("T", 11), "copy 3": ("T", 0),
    "streams": ("T", 4), "ms": ("XT", 0), "rms": ("T", 6), "newton": ("S", 1), "scaled": ("T", 0),
    "stats": ("S", 7), "rstd": ("S", 8), "normalise": ("S", 10),
}
GROUP_OFFSET = (-1, -2, -2, -2)
UNITS = {"XT": 1, "QK": 2, "V": 1, "S": 12, "T": 12, "NT": 2, "OT": 1, "OP": 1, "NM": 1}


def offset(kind, u):
    if kind == "T":
        return -1 if u < 6 else -2
    return {"XT": 1, "QK": 1, "V": 1, "S": 0, "NM": -1, "NT": -2, "OT": -3, "OP": -3}[kind]


class Turn:

    def __init__(self, r, c, looped):
        self.r, self.c, self.looped = r, c, looped

    def runs(self, off):
        return self.looped or 0 <= self.c + off < B

    def at(self, off, per=1, add=0):
        return self.r * (3 * per) + ((self.c + off) * per + add)

    def slot(self, off):
        return (self.c + off) % NSLOT

    def uses(self, off, per=1):
        return self.r * per + ((self.c + off) // NSLOT + 1) * per


def turns(engine, body, first):
    start = 4
    for i in range(first, start):
        body(Turn(0, i, False))
    n = (B - 2 - start) // NSLOT
    with engine.Fori(0, n) as r:
        for k in range(NSLOT):
            body(Turn(r, start + k, True))
    for i in range(start + NSLOT * n, B + 3):
        body(Turn(0, i, False))


def attention(nc, tag, x_in, x_out, w):
    stack_q = nc.dram_tensor(f"{tag}_stack_q", (NSLOT, 2, AUG, H, S), BF16).ap()
    stack_k = nc.dram_tensor(f"{tag}_stack_k", (NSLOT, 2, AUG, H, S), BF16).ap()
    max_rows = nc.dram_tensor(f"{tag}_max_rows", (NSLOT, 2 * 3 * H, S), BF16).ap()
    with ExitStack() as ctx:
        def sb(name, shape, dt=F32):
            return ctx.enter_context(nc.sbuf_tensor(f"{tag}_{name}", shape, dt))

        def ps(name, shape, dt=F32):
            return ctx.enter_context(nc.psum_tensor(f"{tag}_{name}", shape, dt))

        def sem(name):
            return ctx.enter_context(nc.semaphore(f"{tag}_{name}"))

        wqk = sb("wqk", [P, 2 * NC4, P])
        bqk = sb("bqk", [P, 2 * NC4])
        wv = sb("wv", [P, D])
        bv = sb("bv", [P, D])
        wo = sb("wo", [P, D])
        bo = sb("bo", [P, D])
        rope = sb("rope", [P, 2, S])
        norm_w = sb("norm_w", [P, D])
        lam_in = sb("lam_in", [P, 4, D])
        lam_prod = sb("lam_prod", [P, 2, D])
        lam_sum = sb("lam_sum", [P, 2, H])
        lam_exp = sb("lam_exp", [P, 2, H])
        stream_w = sb("stream_w", [P, H, 2])
        ident = sb("ident", [P, P])
        ident16 = sb("ident16", [P, P], BF16)
        mask = sb("mask", [P, 2, P], BF16)
        one_rows = sb("one_rows", [16, 3, H * S // 16], BF16)
        zero_rows = sb("zero_rows", [16, 4, H * S // 16], BF16)
        minus_half = sb("minus_half", [P, QB])

        x = sb("x", [P, NSLOT, QB, D])
        xr = sb("xr", [P, NSLOT, QB, D])
        xrb = sb("xrb", [P, QB, D])
        xo = sb("xo", [P, NSLOT, QB, D])
        stats = sb("stats", [P, QB, 6])
        mean_var = sb("mean_var", [P, QB, 2])
        var_eps = sb("var_eps", [P, QB])
        rstd = sb("rstd", [P, QB])
        xn = sb("xn", [P, QB, D])
        xt = sb("xt", [P, S])
        turned = sb("turned", [P, 2, 2, 2 * S])
        qk = sb("qk", [P, 2, 2 * S])
        left = sb("left", [P, 2, 2 * S])
        parts = sb("parts", [P, 2, 3, 2 * S], BF16)
        qs = sb("qs", [2 * AUG, NSLOT, H, S], BF16)
        kd = sb("kd", [2 * AUG, NSLOT, H, 2, S], BF16)
        v = sb("v", [P, NSLOT, QB, H, VW])
        nmax = sb("nmax", [P, QB, HS])
        nmax_left = sb("nmax_left", [P, QB, HS])
        nmax_parts = sb("nmax_parts", [P, QB, 2, 3, H], BF16)
        nmax_t = sb("nmax_t", [2 * 3 * H, S], BF16)
        prob = sb("prob", [P, NP, 1024])
        o_t = sb("o_t", [P, 4, 2, S])
        rsum = sb("rsum", [P, QB, HS])
        rsum_w = sb("rsum_w", [P, QB, HS])
        o_w = sb("o_w", [P, QB, HS, HD])
        o = sb("o", [P, QB, H, HD])
        o_sq = sb("o_sq", [P, QB, H, HD])
        ms = sb("ms", [P, QB * H])
        ms_eps = sb("ms_eps", [P, QB * H])
        ln_ms = sb("ln_ms", [P, QB * H])
        y0 = sb("y0", [P, QB * H])
        newton = sb("newton", [P, QB * H])
        newton2 = sb("newton2", [P, QB * H])
        rrms = sb("rrms", [P, QB * H])
        o_n = sb("o_n", [P, QB, H, HD])
        o_f = sb("o_f", [P, QB, D])
        of_t = sb("of_t", [P, S])

        ring = ps("ring", [P, 3, 1024])
        o_ps = ps("o_ps", [P, 2, 2, S])

        weights_in = sem("weights_in")
        rows_in = sem("rows_in")
        setup = sem("setup")
        dve_setup = sem("dve_setup")
        lam_ready = sem("lam_ready")
        lam_sums = sem("lam_sums")
        lam_step = sem("lam_step")
        ms_ready = sem("ms_ready")
        x_in_s = [sem(f"x_in{k}") for k in range(NSLOT)]
        xr_in = [sem(f"xr_in{k}") for k in range(NSLOT)]
        stored = sem("stored")
        stack_out = sem("stack_out")
        stack_in = [sem(f"stack_in{k}") for k in range(NSLOT)]
        max_out = sem("max_out")
        max_in = sem("max_in")
        ln_step = sem("ln_step")
        rstd_ready = sem("rstd_ready")
        xn_ready = sem("xn_ready")
        pe = {kind: sem(f"{kind}_computed") for kind in UNITS}
        read = {kind: sem(f"{kind}_read") for kind in UNITS}
        qk_ready = sem("qk_ready")
        hi_ready = sem("hi_ready")
        left_step = sem("left_step")
        mid_ready = sem("mid_ready")
        max_step = sem("max_step")
        masked = sem("masked")
        prob_ready = sem("prob_ready")
        pv_done = sem("pv_done")
        o_copied = sem("o_copied")
        norm_step = sem("norm_step")
        rms_step = sem("rms_step")
        pool_norm = sem("pool_norm")
        NORM = 11

        def wait_unit(engine, turn, kind, n):
            wait(engine, pe[kind], turn.at(offset(kind, n), UNITS[kind], n + 1))

        with nc.Block() as block:

            @block.sync
            def _(sp):
                def load_x(turn):
                    wait_apart(sp, xn_ready, turn.at(2 - NSLOT, 1, 1))
                    sp.dma_start(x[:, turn.slot(2)], x_in[bass.ds(turn.at(2, S), S), :]
                                 .rearrange("(t p) d -> p t d", p=P)).then_inc(x_in_s[turn.slot(2)], 16)

                load_x(Turn(0, -2, False))
                for name, dst in (("wqk", wqk), ("bqk", bqk), ("wv", wv), ("wo", wo), ("rope", rope)):
                    sp.dma_start(dst[:], w[name]).then_inc(weights_in, 16)
                for name, dst in (("bv", bv), ("bo", bo), ("norm_w", norm_w)):
                    sp.dma_start(dst[:], w[name].partition_broadcast(P)).then_inc(weights_in, 16)
                for n, name in enumerate(("lq1", "lk1", "lq2", "lk2")):
                    sp.dma_start(lam_in[:, n], w[name].partition_broadcast(P)).then_inc(weights_in, 16)
                sp.wait_ge(dve_setup, 2)
                for k in range(NSLOT):
                    for s in range(2):
                        sp.dma_start(stack_k[k, s, ROWS:ROWS + 3].rearrange("r h q -> r (h q)")
                                     .rearrange("r (p n) -> p r n", p=16), one_rows[:]).then_inc(rows_in, 16)
                        sp.dma_start(stack_k[k, s, ROWS + 3:AUG].rearrange("r h q -> r (h q)")
                                     .rearrange("r (p n) -> p r n", p=16), zero_rows[:, 0:1]).then_inc(rows_in, 16)
                        sp.dma_start(stack_q[k, s, ROWS:AUG].rearrange("r h q -> r (h q)")
                                     .rearrange("r (p n) -> p r n", p=16), zero_rows[:]).then_inc(rows_in, 16)

                def body(turn):
                    if turn.runs(2) and not (turn.c == -2 and not turn.looped):
                        load_x(turn)
                    if turn.runs(-3):
                        wait_apart(sp, read["OP"], turn.at(-4, 1, 1))
                        sp.dma_start(xr[:, turn.slot(-3)], x_in[bass.ds(turn.at(-3, S), S), :]
                                     .rearrange("(t p) d -> p t d", p=P)).then_inc(xr_in[turn.slot(-3)], 16)
                    if turn.runs(-1):
                        k = turn.slot(-1)
                        wait_apart(sp, read["NM"], turn.at(-1, 1, 1))
                        sp.dma_start(max_rows[k], nmax_t[:]).then_inc(max_out, 16)
                        wait_apart(sp, max_out, turn.at(-1, 16, 16))
                        for s in range(2):
                            sp.dma_start(qs[s * AUG + ROWS:s * AUG + ROWS + 3, k], max_rows[k, 3 * H * s:3 * H * (s + 1)]
                                         .rearrange("(r h) q -> r h q", r=3)).then_inc(max_in, 16)
                    if turn.runs(1):
                        k = turn.slot(1)
                        for n, dst in ((0, stack_q), (1, stack_k)):
                            wait_apart(sp, left_step, turn.at(1, 4, 3 + n))
                            for term, part in enumerate(t[n] for t in TERMS):
                                rows = dst[k, :, term * HD:(term + 1) * HD].rearrange("s d (pp c) q -> s (d pp) (c q)", c=2)
                                sp.dma_start(rows, parts[:, n, part]).then_inc(stack_out, 16)
                        wait_apart(sp, stack_out, turn.at(1, 16 * 2 * len(TERMS), 16 * 2 * len(TERMS)))
                        sp.wait_ge(rows_in, 16 * 6 * NSLOT)
                        wait_apart(sp, pe["T"], turn.at(1 - NSLOT, 12, 12))
                        sp.dma_start(qs[:, k], stack_q[k].rearrange("s r h q -> (s r) h q")).then_inc(stack_in[k], 16)
                        for s in range(2):
                            sp.dma_start(kd[s * AUG:(s + 1) * AUG, k, :, s, :], stack_k[k, s]).then_inc(stack_in[k], 16)
                    if turn.runs(-3):
                        wait_apart(sp, read["OP"], turn.at(-3, 1, 1))
                        wait_apart(sp, stored, turn.at(-3, 16))
                        sp.dma_start(x_out[bass.ds(turn.at(-3, S), S), :].rearrange("(t p) d -> p t d", p=P),
                                     xo[:, turn.slot(-3)]).then_inc(stored, 16)

                turns(sp, body, -1)
                sp.wait_ge(stored, 16 * B)

            @block.gpsimd
            def _(pool):
                nc.gpsimd.memset(ident[:], 0.0)
                nc.gpsimd.memset(mask[:], 0.0)
                nc.gpsimd.memset(minus_half[:], -0.5).then_inc(setup, 1)
                pool.wait_ge(setup, 1)
                nc.gpsimd.affine_select(out=ident[:], in_=ident[:], compare_op=ALU.not_equal, fill=1.0,
                                        base=0, pattern=[[-1, P]], channel_multiplier=1)
                nc.gpsimd.affine_select(out=mask[:], in_=mask[:], compare_op=ALU.is_ge, fill=MASKED,
                                        base=0, pattern=[[0, 2], [-1, P]], channel_multiplier=1).then_inc(setup, 1)

                def ln_rstd(turn):
                    wait(pool, ln_step, turn.at(2, 3, 3))
                    nc.gpsimd.tensor_tensor(rstd[:], var_eps[:], minus_half[:], ALU.pow).then_inc(rstd_ready, 1)

                def low_part(turn, n, what):
                    if not turn.runs(1):
                        return
                    if what == "rotate":
                        wait(pool, read["QK"], turn.at(1, 2, n + 1))
                        wait(pool, left_step, turn.at(0, 4, n + 1))
                        nc.gpsimd.tensor_tensor(qk[:, n], turned[:, n, 0], turned[:, n, 1], ALU.add).then_inc(qk_ready, 1)
                    elif what == "left":
                        wait(pool, hi_ready, turn.at(1, 2, n + 1))
                        nc.gpsimd.tensor_tensor(left[:, n], qk[:, n], parts[:, n, 0], ALU.subtract).then_inc(left_step, 1)
                    else:
                        wait(pool, mid_ready, turn.at(1, 2, n + 1))
                        nc.gpsimd.tensor_tensor(parts[:, n, 2], left[:, n], parts[:, n, 1],
                                                ALU.subtract).then_inc(left_step, 1)

                def causal(turn, u):
                    wait_apart(pool, prob_ready, turn.at(offset("T", u), 12, u + 1))
                    p = prob[:, u % NP]
                    p = p.rearrange("k (a q) -> k a q", q=P) if u % 3 == 2 else \
                        p.rearrange("k (a q) -> k a q", q=S)[:, :, 0:P]
                    nc.gpsimd.affine_select(out=p, in_=p, compare_op=ALU.is_ge, fill=0.0, base=0,
                                            pattern=[[0, p.shape[1]], [1, P]], channel_multiplier=-1).then_inc(masked, 1)

                def streams(turn):
                    wait(pool, norm_step, turn.at(-2, NORM, 6))
                    ow = o_w[:].rearrange("p b (h s) d -> p (b h) s d", s=2)
                    of = o[:].rearrange("p b h d -> p (b h) d")
                    nc.gpsimd.tensor_tensor(of, ow[:, :, 0], ow[:, :, 1], ALU.add).then_inc(pool_norm, 1)
                    wait(pool, pool_norm, turn.at(-2, 5, 1))
                    of = o[:].rearrange("p b h d -> p (b h d)")
                    nc.gpsimd.tensor_tensor(o_sq[:].rearrange("p b h d -> p (b h d)"), of, of, ALU.mult).then_inc(pool_norm, 1)

                def scaled(turn):
                    wait(pool, norm_step, turn.at(-3, NORM, NORM))
                    nc.gpsimd.tensor_tensor(o_n[:].rearrange("p b h d -> p (b h) d"), o[:].rearrange("p b h d -> p (b h) d"),
                                            rrms[:].unsqueeze(2).to_broadcast([P, QB * H, HD]), ALU.mult).then_inc(pool_norm, 1)
                    wait(pool, pool_norm, turn.at(-3, 5, 3))
                    wait(pool, pe["OT"], turn.at(-4, 1, 1))
                    nc.gpsimd.tensor_tensor(o_f[:], o_n[:].rearrange("p b h d -> p b (h d)"),
                                            norm_w[:].unsqueeze(1).to_broadcast([P, QB, D]), ALU.mult).then_inc(pool_norm, 1)
                    wait(pool, xr_in[turn.slot(-3)], turn.uses(-3, 16))
                    wait(pool, read["OP"], turn.at(-4, 1, 1))
                    nc.gpsimd.tensor_tensor(xrb[:], xr[:, turn.slot(-3)], bo[:].unsqueeze(1).to_broadcast([P, QB, D]),
                                            ALU.add).then_inc(pool_norm, 1)

                pool.wait_ge(dve_setup, 6)
                pool.wait_ge(weights_in, 16 * 12)

                def body(turn):
                    for kind, u in ORDER:
                        if kind == "T" and turn.runs(offset(kind, u)):
                            causal(turn, u)
                        for n in range(2):
                            for what in ("rotate", "left", "low"):
                                if (kind, u) == AFTER[f"{what} {n}"]:
                                    low_part(turn, n, what)
                        if (kind, u) == AFTER["scaled"] and turn.runs(-3):
                            scaled(turn)
                        if (kind, u) == AFTER["streams"] and turn.runs(-2):
                            streams(turn)
                        if (kind, u) == AFTER["rstd"] and turn.runs(2):
                            ln_rstd(turn)

                ln_rstd(Turn(0, -2, False))
                turns(pool, body, -1)

            @block.scalar
            def _(act):
                act.wait_ge(dve_setup, 3)
                nc.scalar.activation(ln_ms[:], y0[:], ACT.Ln).then_inc(lam_ready, 1)
                act.wait_ge(lam_sums, 1)
                nc.scalar.activation(lam_exp[:], lam_sum[:], ACT.Exp).then_inc(lam_ready, 1)

                def body(turn):
                    for kind, u in ORDER:
                        if kind == "XT" and turn.runs(1):
                            wait_unit(act, turn, kind, u)
                            wait(act, pe["V"], turn.at(0, 1, 1))
                            nc.scalar.activation(xt[:], ring[:, ORDER.index((kind, u)) % 3, 0:S],
                                                 ACT.Copy).then_inc(read["XT"], 1)
                        if kind == "T" and turn.runs(offset(kind, u)):
                            wait_unit(act, turn, kind, u)
                            wait(act, pv_done, turn.at(offset(kind, u), 4, (u - NP) // 3 + 1))
                            nc.scalar.activation(prob[:, u % NP], ring[:, ORDER.index((kind, u)) % 3], ACT.Exp,
                                                 scale=SCALE).then_inc(prob_ready, 1)
                        for n in range(2):
                            if (kind, u) == AFTER[f"high {n}"] and turn.runs(1):
                                wait(act, qk_ready, turn.at(1, 2, n + 1))
                                wait(act, stack_out, turn.at(0, 16 * 2 * len(TERMS), 16 * 2 * len(TERMS)))
                                nc.scalar.activation(parts[:, n, 0], qk[:, n], ACT.Copy).then_inc(hi_ready, 1)
                            if (kind, u) == AFTER[f"mid {n}"] and turn.runs(1):
                                wait(act, left_step, turn.at(1, 4, n + 1))
                                nc.scalar.activation(parts[:, n, 1], left[:, n], ACT.Copy).then_inc(mid_ready, 1)
                        for g in range(4):
                            if (kind, u) == AFTER[f"copy {g}"] and turn.runs(GROUP_OFFSET[g]):
                                o_copy(turn, GROUP_OFFSET[g], g)
                        if (kind, u) == AFTER["rms"] and turn.runs(-3):
                            wait(act, norm_step, turn.at(-3, NORM, 7))
                            nc.scalar.activation(ln_ms[:], ms_eps[:], ACT.Ln).then_inc(rms_step, 1)
                            wait(act, rms_step, turn.at(-3, 2, 1))
                            nc.scalar.activation(y0[:], ln_ms[:], ACT.Exp, scale=-0.5).then_inc(rms_step, 1)
                        if kind == "OT" and turn.runs(-3):
                            wait_unit(act, turn, kind, u)
                            wait(act, pe["OP"], turn.at(-4, 1, 1))
                            nc.scalar.activation(of_t[:], ring[:, ORDER.index((kind, u)) % 3, 0:S],
                                                 ACT.Copy).then_inc(read["OT"], 1)
                        if kind == "NM" and turn.runs(-1):
                            wait_unit(act, turn, kind, u)
                            wait(act, max_out, turn.at(-2, 16, 16))
                            nc.scalar.activation(nmax_t[:], ring[0:2 * 3 * H, ORDER.index((kind, u)) % 3, 0:S // 2]
                                                 .bitcast(BF16), ACT.Copy).then_inc(read["NM"], 1)

                def o_copy(turn, off, g):
                    wait(act, pv_done, turn.at(off, 4, g + 1))
                    wait(act, pe["NT"], turn.at(off - 1, 2, 2))
                    nc.scalar.activation(o_t[:, g], o_ps[:, g % 2], ACT.Copy).then_inc(o_copied, 1)

                turns(act, body, -1)

            @block.vector
            def _(dve):
                nc.vector.memset(one_rows[:], 1.0).then_inc(dve_setup, 1)
                nc.vector.memset(zero_rows[:], 0.0).then_inc(dve_setup, 1)
                nc.vector.memset(y0[:], 1.0).then_inc(dve_setup, 1)
                nc.vector.memset(v[:], 0.0).then_inc(dve_setup, 1)
                nc.vector.memset(kd[:].bitcast(U32), 0).then_inc(dve_setup, 1)
                dve.wait_ge(dve_setup, 4)
                nc.vector.memset(v[:, :, :, :, HD:HD + 1], 1.0).then_inc(dve_setup, 1)
                dve.wait_ge(setup, 2)
                nc.vector.tensor_copy(ident16[:], ident[:]).then_inc(dve_setup, 1)
                dve.wait_ge(weights_in, 16 * 12)
                for n in range(2):
                    last = nc.vector.tensor_tensor(lam_prod[:, n], lam_in[:, 2 * n], lam_in[:, 2 * n + 1], ALU.mult)
                last.then_inc(lam_step, 1)
                dve.wait_ge(lam_step, 1)
                nc.vector.tensor_reduce(lam_sum[:], lam_prod[:].rearrange("p n (h d) -> p n h d", d=HD), AX.X,
                                        ALU.add).then_inc(lam_sums, 1)
                nc.vector.memset(stream_w[:, :, 0], 1.0)
                nc.vector.tensor_scalar(norm_w[:], norm_w[:], 1.0 - LAMBDA_INIT, None, ALU.mult).then_inc(lam_step, 1)
                dve.wait_ge(lam_ready, 2)
                nc.vector.scalar_tensor_tensor(out=stream_w[:, :, 1], in0=lam_exp[:, 1], scalar=-LAMBDA_INIT,
                                               in1=lam_exp[:, 0], op0=ALU.add, op1=ALU.subtract).then_inc(lam_step, 1)
                dve.wait_ge(lam_step, 3)

                def ln_stats(turn):
                    wait(dve, x_in_s[turn.slot(2)], turn.uses(2, 16))
                    for t in range(QB):
                        last = nc.vector.bn_stats(stats[:, t], x[:, turn.slot(2), t])
                    last.then_inc(ln_step, 1)
                    wait_apart(dve, ln_step, turn.at(2, 3, 1))
                    for t in range(QB):
                        last = nc.vector.bn_aggr(mean_var[:, t], stats[:, t])
                    last.then_inc(ln_step, 1)
                    wait(dve, ln_step, turn.at(2, 3, 2))
                    nc.vector.tensor_scalar(var_eps[:], mean_var[:, :, 1], LN_EPS, None, ALU.add).then_inc(ln_step, 1)

                def normalise(turn):
                    wait(dve, rstd_ready, turn.at(2, 1, 1))
                    wait(dve, pe["XT"], turn.at(1, 1, 1))
                    for t in range(QB):
                        last = nc.vector.tensor_scalar(xn[:, t], x[:, turn.slot(2), t], mean_var[:, t, 0:1],
                                                       rstd[:, t:t + 1], ALU.subtract, ALU.mult)
                    last.then_inc(xn_ready, 1)

                def body(turn):
                    def norm(instruction, off, n):
                        instruction.then_inc(norm_step, 1)
                        wait(dve, norm_step, turn.at(off, NORM, n))

                    for pos, (kind, u) in enumerate(ORDER):
                        if not turn.runs(offset(kind, u)):
                            pass
                        elif kind == "QK":
                            wait_unit(dve, turn, kind, u)
                            wait(dve, qk_ready, turn.at(0, 2, u + 1))
                            for partner in range(2):
                                for c in range(2):
                                    col = (2 * partner + c) * S
                                    n = 4 * u + 2 * partner + c
                                    last = nc.vector.scalar_tensor_tensor(
                                        out=turned[:, u, partner, c * S:(c + 1) * S], in0=ring[:, pos % 3, col:col + S],
                                        scalar=bqk[:, n:n + 1], in1=rope[:, partner], op0=ALU.add, op1=ALU.mult)
                            last.then_inc(read["QK"], 1)
                        elif kind == "V":
                            wait_unit(dve, turn, kind, u)
                            wait(dve, pv_done, turn.at(1 - NSLOT, 4, 4))
                            for t in range(QB):
                                last = nc.vector.tensor_tensor(
                                    v[:, turn.slot(1), t, :, 0:HD],
                                    ring[:, pos % 3, t * D:(t + 1) * D].rearrange("p (h d) -> p h d", d=HD),
                                    bv[:].rearrange("p (h d) -> p h d", d=HD), ALU.add)
                            last.then_inc(read["V"], 1)
                        elif kind == "S":
                            wait_unit(dve, turn, kind, u)
                            if u == 0:
                                wait(dve, max_step, turn.at(-1, 4, 4))
                            b, n, width = (0, 8 * u, P) if u < 4 else (1, 4 * (u - 4), S)
                            cnt = 1024 // width
                            nc.vector.tensor_reduce(nmax[:, b, n:n + cnt], ring[:, pos % 3]
                                                    .rearrange("p (a k) -> p a k", k=width), AX.X, ALU.max,
                                                    negate=True).then_inc(read["S"], 1)
                        elif kind == "NT":
                            wait_unit(dve, turn, kind, u)
                            got = ring[:, pos % 3].rearrange("p (a c) -> p a c", c=VW)
                            wait(dve, pool_norm, turn.at(-3, 5, 1))
                            norm(nc.vector.reciprocal(rsum[:, u], got[:, :, HD]), -2, 3 * u + 1)
                            norm(nc.vector.tensor_tensor(rsum_w[:, u], rsum[:, u],
                                                         stream_w[:].rearrange("p h s -> p (h s)"), ALU.mult), -2, 3 * u + 2)
                            nc.vector.tensor_tensor(o_w[:, u], got[:, :, 0:HD],
                                                    rsum_w[:, u].unsqueeze(2).to_broadcast([P, HS, HD]),
                                                    ALU.mult).then_inc(norm_step, 1)
                        elif kind == "OP":
                            wait_unit(dve, turn, kind, u)
                            wait(dve, pool_norm, turn.at(-3, 5, 5))
                            wait(dve, stored, turn.at(-4, 16, 16))
                            nc.vector.tensor_tensor(xo[:, turn.slot(-3)], ring[:, pos % 3, 0:S]
                                                    .rearrange("p (t d) -> p t d", d=D), xrb[:], ALU.add).then_inc(read["OP"], 1)
                        if (kind, u) == AFTER["ms"] and turn.runs(-3):
                            wait(dve, pool_norm, turn.at(-3, 5, 2))
                            nc.vector.tensor_reduce(ms[:], o_sq[:].rearrange("p b h d -> p (b h) d"), AX.X,
                                                    ALU.add).then_inc(ms_ready, 1)
                            wait(dve, ms_ready, turn.at(-3, 1, 1))
                            nc.vector.tensor_scalar(ms_eps[:], ms[:], 1.0 / HD, RMS_EPS, ALU.mult,
                                                    ALU.add).then_inc(norm_step, 1)
                        if (kind, u) == AFTER["newton"] and turn.runs(-3):
                            wait(dve, rms_step, turn.at(-3, 2, 2))
                            norm(nc.vector.tensor_tensor(newton[:], ms_eps[:], y0[:], ALU.mult), -3, 8)
                            norm(nc.vector.tensor_tensor(newton2[:], newton[:], y0[:], ALU.mult), -3, 9)
                            norm(nc.vector.tensor_scalar(newton[:], newton2[:], -0.5, 1.5, ALU.mult, ALU.add), -3, 10)
                            nc.vector.tensor_tensor(rrms[:], newton[:], y0[:], ALU.mult).then_inc(norm_step, 1)
                        if (kind, u) == AFTER["stats"] and turn.runs(2):
                            ln_stats(turn)
                        if (kind, u) == AFTER["normalise"] and turn.runs(2):
                            normalise(turn)
                        if (kind, u) == ("S", 11) and turn.runs(0):
                            def part(instruction, n):
                                instruction.then_inc(max_step, 1)
                                wait(dve, max_step, turn.at(0, 4, n))

                            def rows(n):
                                return nmax_parts[:, :, :, n].rearrange("p b s h -> p b h s")

                            def flat(t):
                                return t[:].rearrange("p b (h s) -> p b h s", s=2)

                            wait(dve, read["S"], turn.at(0, 12, 12))
                            wait(dve, pe["NM"], turn.at(-1, 1, 1))
                            part(nc.vector.tensor_copy(rows(0), flat(nmax)), 1)
                            part(nc.vector.tensor_tensor(flat(nmax_left), flat(nmax), rows(0), ALU.subtract), 2)
                            part(nc.vector.tensor_copy(rows(1), flat(nmax_left)), 3)
                            nc.vector.tensor_tensor(rows(2), flat(nmax_left), rows(1), ALU.subtract).then_inc(max_step, 1)

                first = Turn(0, -2, False)
                ln_stats(first)
                normalise(first)
                turns(dve, body, -1)

            @block.tensor
            def _(te):
                te.wait_ge(dve_setup, 7)
                te.wait_ge(weights_in, 16 * 12)

                def free(turn, pos):
                    back = pos - 3
                    c = turn.c
                    while True:
                        if back < 0:
                            back, c = back + len(ORDER), c - 1
                        if not turn.looped and c < -1:
                            return
                        kind, u = ORDER[back]
                        before = Turn(turn.r, c, turn.looped)
                        if before.runs(offset(kind, u)):
                            break
                        back -= 3
                    if kind == "T":
                        wait(te, prob_ready, before.at(offset(kind, u), 12, u + 1))
                    elif kind == "NT":
                        wait(te, norm_step, before.at(offset(kind, u), NORM, 3 * u + 3))
                    else:
                        wait(te, read[kind], before.at(offset(kind, u), UNITS[kind], u + 1))

                def mm(out, lhs, rhs, start=True, stop=True):
                    return nc.tensor.matmul(out, lhs, rhs, start=start, stop=stop)

                def weigh(turn, off, g):
                    wait(te, masked, turn.at(off, 12, 3 * g + 3))
                    wait(te, o_copied, turn.at(off, 4, g - 1))
                    k = turn.slot(off)
                    for j in range(2):
                        for b in range(2):
                            for i in range(4):
                                h = (8 * g + 4 * j + i) // 2
                                p = prob[:, (3 * g + j) % NP, i * S:(i + 1) * S] if b == 0 else \
                                    prob[:, (3 * g + 2) % NP, (4 * j + i) * P:(4 * j + i + 1) * P]
                                last = nc.tensor.matmul(o_ps[VW * i:VW * (i + 1), g % 2, j, b * P:S], v[:, k, b, h], p,
                                                        start=(b == 0), stop=(b == 1), tile_position=(0, VW * i))
                    last.then_inc(pv_done, 1)

                def body(turn):
                    for pos, (kind, u) in enumerate(ORDER):
                        buf = ring[:, pos % 3]
                        if turn.runs(offset(kind, u)):
                            free(turn, pos)
                            if kind == "XT":
                                wait(te, xn_ready, turn.at(1, 1, 1))
                                for t in range(QB):
                                    last = nc.tensor.transpose(buf[:, t * P:(t + 1) * P], xn[:, t], ident[:])
                            elif kind == "QK":
                                wait(te, read["XT"], turn.at(1, 1, 1))
                                for n in range(4):
                                    last = mm(buf[:, n * S:(n + 1) * S], wqk[:, 4 * u + n], xt[:])
                            elif kind == "V":
                                for t in range(QB):
                                    last = mm(buf[:, t * D:(t + 1) * D], xt[:, t * P:(t + 1) * P], wv[:])
                            elif kind == "S":
                                k = turn.slot(0)
                                if u == 0:
                                    wait(te, stack_in[k], turn.uses(0, 48))
                                b, h0, width = (0, 4 * u, P) if u < 4 else (1, 2 * (u - 4), S)
                                for n in range(1024 // (2 * width)):
                                    out = buf[:, n * 2 * width:(n + 1) * 2 * width].rearrange("q (s k) -> q s k", s=2)
                                    mm(out, qs[:, k, h0 + n, b * P:(b + 1) * P], kd[:, k, h0 + n, :, 0:width], stop=False)
                                    last = mm(out[:, :, b * P:(b + 1) * P], ident16[:], mask[:], start=False)
                            elif kind == "T":
                                k = turn.slot(offset(kind, u))
                                if u == 0:
                                    wait(te, max_in, turn.at(-1, 32, 32))
                                g, n = divmod(u, 3)
                                for i in range(8 if n == 2 else 4):
                                    hs = 8 * g + (i if n == 2 else 4 * n + i)
                                    b = 1 if n == 2 else 0
                                    q0 = b * P
                                    last = mm(buf[:, i * (S - q0):(i + 1) * (S - q0)],
                                              kd[:, k, hs // 2, hs % 2, b * P:(b + 1) * P], qs[:, k, hs // 2, q0:S])
                            elif kind == "NT":
                                wait(te, o_copied, turn.at(-2, 4, 4))
                                for n in range(8):
                                    last = nc.tensor.transpose(buf[:, n * P:(n + 1) * P],
                                                               o_t[:, n // 2, n % 2, u * P:(u + 1) * P], ident[:])
                            elif kind == "OT":
                                wait(te, pool_norm, turn.at(-3, 5, 4))
                                for t in range(QB):
                                    last = nc.tensor.transpose(buf[:, t * P:(t + 1) * P], o_f[:, t], ident[:])
                            elif kind == "OP":
                                wait(te, read["OT"], turn.at(-3, 1, 1))
                                for t in range(QB):
                                    last = mm(buf[:, t * D:(t + 1) * D], of_t[:, t * P:(t + 1) * P], wo[:])
                            elif kind == "NM":
                                wait(te, max_step, turn.at(-1, 4, 4))
                                for b in range(QB):
                                    last = nc.tensor.transpose(
                                        buf[0:2 * 3 * H, b * P // 2:(b + 1) * P // 2].bitcast(BF16),
                                        nmax_parts[:, b].rearrange("p s r h -> p (s r h)"), ident16[:])
                            last.then_inc(pe[kind], 1)
                        for g in range(4):
                            if (kind, u) == AFTER[f"weigh {g}"] and turn.runs(GROUP_OFFSET[g]):
                                weigh(turn, GROUP_OFFSET[g], g)

                turns(te, body, -1)


def layout(L0_attn_x, L0_attn_Wq, L0_attn_bq, L0_attn_Wk, L0_attn_bk, L0_attn_Wv, L0_attn_bv, L0_attn_Wo, L0_attn_bo,
           L0_attn_head_norm_w, L0_attn_lq1, L0_attn_lk1, L0_attn_lq2, L0_attn_lk2, L0_ffn_gate_w,
           L0_ffn_balance_bias, L0_ffn_w1, L0_ffn_w2):
    c = np.ascontiguousarray
    order = np.array([[[[(2 * pp + ch) * 2 * HD + s * HD + d for pp in range(H // 2)] for d in range(HD)]
                       for s in range(2)] for ch in range(2)]).reshape(2, P)
    partner = np.where(order % HD < HD // 2, order + HD // 2, order - HD // 2)
    rows = np.stack([order, partner])
    wqk = np.stack([L0_attn_Wq[rows], L0_attn_Wk[rows]])
    bqk = np.stack([L0_attn_bq[rows], L0_attn_bk[rows]])
    half = HD // 2
    freq = np.float32(1.0) / np.power(np.float32(10000.0), np.arange(half, dtype=np.float32) / np.float32(half))
    angle = (np.arange(S, dtype=np.float32)[None, :] * freq[:, None]).astype(np.float64)
    d = order[0] % HD
    cos = np.cos(angle)[d % half]
    sin = np.sin(angle)[d % half] * np.where(d < half, -1.0, 1.0)[:, None]
    return {
        "x": c(L0_attn_x.reshape(T, D)),
        "gate_w": c(L0_ffn_gate_w.T),
        "gate_b": c(L0_ffn_balance_bias),
        "w1": c(L0_ffn_w1.reshape(E * EH, D).T),
        "w2": c(L0_ffn_w2.transpose(0, 2, 1).reshape(HC, P, D).transpose(1, 0, 2).reshape(P, HC * D)),
        "wqk": c(wqk.reshape(2 * NC4, P, D).transpose(2, 0, 1)),
        "bqk": c(bqk.reshape(2 * NC4, P).T),
        "wv": c(L0_attn_Wv.T),
        "wo": c(L0_attn_Wo.T),
        "bv": c(L0_attn_bv),
        "bo": c(L0_attn_bo),
        "norm_w": c(L0_attn_head_norm_w.reshape(D)),
        "lq1": c(L0_attn_lq1.reshape(D)), "lk1": c(L0_attn_lk1.reshape(D)),
        "lq2": c(L0_attn_lq2.reshape(D)), "lk2": c(L0_attn_lk2.reshape(D)),
        "rope": c(np.stack([cos, sin], 1).astype(np.float32)),
    }


def build(nc, a, out):
    x1 = nc.dram_tensor("x1", (T, D), F32).ap()
    x2 = nc.dram_tensor("x2", (T, D), F32).ap()
    ffn(nc, "ffn1", a["x"], x1, a)
    attention(nc, "att", x1, x2, a)
    ffn(nc, "ffn2", x2, out, a)



def kernel(**inputs):
    import numpy as _np
    import concourse.bacc as _bacc
    from concourse.bass_utils import run_bass_kernel_spmd as _run

    arrays = layout(**{k: _np.asarray(v) for k, v in inputs.items()})
    nc = _bacc.Bacc("TRN2", target_bir_lowering=False, num_devices=1)
    aps = {n: nc.dram_tensor(n, a.shape, mybir.dt.from_np(a.dtype), kind="ExternalInput").ap()
           for n, a in arrays.items()}
    out = nc.dram_tensor("out", (T, D), F32, kind="ExternalOutput").ap()
    build(nc, aps, out)
    r = _run(nc, [arrays], core_ids=[0])
    return r.results[0]["out"].reshape(B, S, D)
```
